# Optimizing a Trainium2 kernel written in Bass

```python
import numpy as np
import jax
import jax.numpy as jnp

def _softmax(x, axis=-1):
    return jax.nn.softmax(x, axis=axis)

def _gelu(x):
    return jax.nn.gelu(x, approximate=True)

def _silu(x):
    return jax.nn.silu(x)

def _sigmoid(x):
    return jax.nn.sigmoid(x)

def _layernorm(x, axis=-1, eps=1e-05):
    m = jnp.mean(x, axis=axis, keepdims=True)
    v = jnp.var(x, axis=axis, keepdims=True)
    return (x - m) / jnp.sqrt(v + eps)

def _scatter_add(tgt, idx, src, axis=0):
    return tgt.at[idx].add(src)

def _segment_sum(src, seg, n):
    return jax.ops.segment_sum(src, seg, n)
kernel_name = 'mk_audio_tower_d1_tok_audfeat256_r4_673788'

def setup_inputs(seed: int=0):
    np.random.seed(seed)
    _w = jnp.asarray

    def _rec_inputs():
        import jax
        import jax.numpy as jnp
        _rk = jax.random.key(seed)
        x = 7.22013e-05 + 1.00017 * jax.random.normal(jax.random.fold_in(_rk, 1), (64, 256, 64), jnp.float32)
        return x
    x = _rec_inputs()

    def _L0_tok_setup():
        import jax, jax.numpy as jnp
        import numpy as np
        WIN = 9
        key = jax.random.key(seed)
        ks = jax.random.split(key, 4)
        N, L, C, U = (8, 1024, 64, 64)
        x = jax.random.normal(ks[0], (N, L, C), dtype=jnp.float32)
        W_qry = jax.random.normal(ks[1], (C, U), dtype=jnp.float32) * 0.05
        W_key = jax.random.normal(ks[2], (C, U), dtype=jnp.float32) * 0.05
        v = jax.random.normal(ks[3], (U,), dtype=jnp.float32) * 0.05
        b = jnp.zeros((U,), dtype=jnp.float32)
        return {'x': x, 'W_qry': W_qry, 'W_key': W_key, 'v': v, 'b': b}
    _L0_tok_all = _L0_tok_setup()
    _L0_tok_in = {k: v for k, v in _L0_tok_all.items() if k in ('W_qry', 'W_key', 'v', 'b')}
    del _L0_tok_all

    def _L0_attn_setup():
        import jax, jax.numpy as jnp
        import numpy as np
        IN_C = 64
        HID_C = 64
        HEADS = 8
        SCALE = 1.0 / np.sqrt(HID_C / HEADS).astype(np.float32)
        key = jax.random.key(seed)
        k_v, k_q, k_k, k_w, k_o, k_b = jax.random.split(key, 6)
        B, S = (4, 512)
        lim_in = 1.0 / np.sqrt(IN_C)
        lim_out = 1.0 / np.sqrt(IN_C * HEADS)
        v = jax.random.normal(k_v, (B, S, IN_C), dtype=jnp.float32)
        WQ = jax.random.uniform(k_q, (IN_C, IN_C * HEADS), jnp.float32, -lim_in, lim_in)
        WK = jax.random.uniform(k_k, (IN_C, IN_C * HEADS), jnp.float32, -lim_in, lim_in)
        WV = jax.random.uniform(k_w, (IN_C, IN_C * HEADS), jnp.float32, -lim_in, lim_in)
        Wout = jax.random.uniform(k_o, (IN_C * HEADS, HID_C), jnp.float32, -lim_out, lim_out)
        bout = jax.random.uniform(k_b, (HID_C,), jnp.float32, -lim_out, lim_out)
        return {'v': v, 'WQ': WQ, 'WK': WK, 'WV': WV, 'Wout': Wout, 'bout': bout}
    _L0_attn_all = _L0_attn_setup()
    _L0_attn_in = {k: v for k, v in _L0_attn_all.items() if k in ('WQ', 'WK', 'WV', 'Wout', 'bout')}
    del _L0_attn_all

    def _L0_ffn_setup():
        import jax, jax.numpy as jnp
        import numpy as np
        B, S, D, H, E, K = (8, 2048, 64, 256, 8, 2)
        key = jax.random.key(seed)
        ks = jax.random.split(key, 7)
        s_in = 1.0 / np.sqrt(D)
        s_hid = 1.0 / np.sqrt(H)
        return {'x': jax.random.normal(ks[0], (B, S, D), dtype=jnp.float32), 'Wg': jax.random.uniform(ks[1], (E, D), jnp.float32, -s_in, s_in), 'bg': jax.random.uniform(ks[2], (E,), jnp.float32, -s_in, s_in), 'W1': jax.random.uniform(ks[3], (E, H, D), jnp.float32, -s_in, s_in), 'b1': jax.random.uniform(ks[4], (E, H), jnp.float32, -s_in, s_in), 'W2': jax.random.uniform(ks[5], (E, D, H), jnp.float32, -s_hid, s_hid), 'b2': jax.random.uniform(ks[6], (E, D), jnp.float32, -s_hid, s_hid)}
    _L0_ffn_all = _L0_ffn_setup()
    _L0_ffn_in = {k: v for k, v in _L0_ffn_all.items() if k in ('Wg', 'bg', 'W1', 'b1', 'W2', 'b2')}
    del _L0_ffn_all
    return {'x': x, 'L0_tok_W_qry': _L0_tok_in['W_qry'], 'L0_tok_W_key': _L0_tok_in['W_key'], 'L0_tok_v': _L0_tok_in['v'], 'L0_tok_b': _L0_tok_in['b'], 'L0_attn_WQ': _L0_attn_in['WQ'], 'L0_attn_WK': _L0_attn_in['WK'], 'L0_attn_WV': _L0_attn_in['WV'], 'L0_attn_Wout': _L0_attn_in['Wout'], 'L0_attn_bout': _L0_attn_in['bout'], 'L0_ffn_Wg': _L0_ffn_in['Wg'], 'L0_ffn_bg': _L0_ffn_in['bg'], 'L0_ffn_W1': _L0_ffn_in['W1'], 'L0_ffn_b1': _L0_ffn_in['b1'], 'L0_ffn_W2': _L0_ffn_in['W2'], 'L0_ffn_b2': _L0_ffn_in['b2']}

def reference(x, L0_tok_W_qry, L0_tok_W_key, L0_tok_v, L0_tok_b, L0_attn_WQ, L0_attn_WK, L0_attn_WV, L0_attn_Wout, L0_attn_bout, L0_ffn_Wg, L0_ffn_bg, L0_ffn_W1, L0_ffn_b1, L0_ffn_W2, L0_ffn_b2):
    import jax
    import jax.numpy as jnp

    def _L0_tok_ref(x, W_qry, W_key, v, b):
        import jax, jax.numpy as jnp
        import numpy as np
        WIN = 9
        N, L, C = x.shape
        n_w = L - WIN + 1
        idx = jnp.arange(n_w)[:, None] + jnp.arange(WIN)[None, :]
        x_win = x[:, idx]
        x_ctr = x[:, WIN // 2:WIN // 2 + n_w]
        key = jnp.einsum('nwsc,cu->nwsu', x_win, W_key)
        qry = jnp.einsum('nwc,cu->nwu', x_ctr, W_qry)
        score = jnp.einsum('nwsu,u->nws', jnp.tanh(qry[:, :, None, :] + key + b), v)
        weight = jax.nn.softmax(score, axis=2)
        out = jnp.einsum('nwsc,nws->nwc', x_win, weight)
        return out

    def _L0_attn_ref(v, WQ, WK, WV, Wout, bout):
        import jax, jax.numpy as jnp
        import numpy as np
        IN_C = 64
        HID_C = 64
        HEADS = 8
        SCALE = 1.0 / np.sqrt(HID_C / HEADS).astype(np.float32)
        B, S, C = v.shape
        H = HEADS
        q = (v @ WQ).reshape(B, S, H, C)
        k = (v @ WK).reshape(B, S, H, C)
        val = (v @ WV).reshape(B, S, H, C)
        scores = jnp.einsum('bshc,bthc->bsth', q, k) * SCALE
        A = jax.nn.softmax(scores, axis=2)
        u = jnp.einsum('bsth,bthc->bshc', A, val).reshape(B, S, H * C)
        return u @ Wout + bout

    def _L0_ffn_ref(x, Wg, bg, W1, b1, W2, b2):
        import jax, jax.numpy as jnp
        import numpy as np
        B, S, D, H, E, K = (8, 2048, 64, 256, 8, 2)
        gate_scores = jnp.einsum('bsd,ed->bse', x, Wg) + bg
        topk_scores, topk_idx = jax.lax.top_k(gate_scores, K)
        topk_probs = jax.nn.softmax(topk_scores, axis=-1)
        combine = jnp.sum(topk_probs[..., None] * jax.nn.one_hot(topk_idx, E, dtype=x.dtype), axis=-2)
        out = jnp.zeros_like(x)
        for e in range(E):
            h = jax.nn.relu(jnp.einsum('bsd,hd->bsh', x, W1[e]) + b1[e])
            y = jnp.einsum('bsh,dh->bsd', h, W2[e]) + b2[e]
            out = out + combine[..., e:e + 1] * y
        return out
    h = _L0_tok_ref(x, L0_tok_W_qry, L0_tok_W_key, L0_tok_v, L0_tok_b)
    h = h + _L0_attn_ref(_layernorm(h, axis=-1), L0_attn_WQ, L0_attn_WK, L0_attn_WV, L0_attn_Wout, L0_attn_bout)
    h = h + _L0_ffn_ref(_layernorm(h, axis=-1), L0_ffn_Wg, L0_ffn_bg, L0_ffn_W1, L0_ffn_b1, L0_ffn_W2, L0_ffn_b2)
    return h

_drawn_inputs = setup_inputs


def setup_inputs(seed=0):
    import zlib

    import numpy as np

    out = dict(_drawn_inputs(seed))
    spreads = {'L0_tok_b': (0.0, 0.1)}
    factors = {}
    for name, (base, spread) in spreads.items():
        noise = np.random.default_rng([zlib.crc32(name.encode()), seed]).standard_normal(out[name].shape)
        drawn = base * np.exp(spread * noise) if base else spread * noise
        out[name] = jnp.asarray(drawn.astype(out[name].dtype))
    for name, factor in factors.items():
        out[name] = (out[name] * factor).astype(out[name].dtype)
    return out
```

```python
import concourse.bass as bass
import concourse.mybir as mybir
import numpy as np
from contextlib import ExitStack

F32 = mybir.dt.float32
F32R = mybir.dt.float32r
BF16 = mybir.dt.bfloat16
I32 = mybir.dt.int32
ALU = mybir.AluOpType
ACT = mybir.ActivationFunctionType
AX = mybir.AxisListType

BATCH, LENGTH, C = 64, 256, 64
WIN = 9
TOKENS = LENGTH - WIN + 1
HALF = TOKENS // 2
PAIR = 2 * TOKENS
HEADS, HP = 8, 4
EXPERTS, HID = 8, 256
EP = EXPERTS // 2
PAIRS = BATCH // 2
QUARTER = 63
PADDED = 4 * QUARTER
EPS = 1e-5
ATTN_SCALE = float(np.float32(1.0) / np.sqrt(np.float32(8.0)).astype(np.float32))
RSQRT_GUESS = 0x5F3759DF

GLANCE, WINDOW, GRAM, ATTEND, SETTLE, MIX = "glance", "window", "gram", "attend", "settle", "mix"
LAG = {GLANCE: 0, WINDOW: 1, GRAM: 1, ATTEND: 2, SETTLE: 3, MIX: 4}
TURNS = PAIRS + LAG[MIX]
STEADY = LAG[MIX]
LOOP_FROM, LOOP_TO = STEADY + 2, PAIRS

BIG_ORDER = ([("un0", SETTLE), ("l1_0", MIX), ("un1", SETTLE), ("l1_1", MIX), ("l1_2", MIX), ("ub0", SETTLE),
              ("l1_3", MIX), ("ub1", SETTLE), ("l1_4", MIX), ("l1_5", MIX), ("l1_6", MIX), ("l1_7", MIX),
              ("yn0", MIX), ("yn1", MIX), ("g0", GRAM), ("g1", GRAM), ("s0", ATTEND), ("s1", ATTEND),
              ("mx0", GRAM), ("s2", ATTEND), ("mx1", GRAM), ("s3", ATTEND), ("mx2", GRAM), ("s4", ATTEND),
              ("mx3", GRAM), ("s5", ATTEND), ("mx4", GRAM), ("s6", ATTEND), ("mx5", GRAM), ("s7", ATTEND),
              ("mx6", GRAM), ("mx7", GRAM)])
SUM_ORDER = [("l2_0", MIX), ("l2_1", MIX), ("l2_2", MIX), ("l2_3", MIX),
             ("av0", ATTEND), ("av1", ATTEND), ("av2", ATTEND), ("av3", ATTEND)]
TOK_ORDER = [("sc", WINDOW), ("scn", WINDOW), ("et", WINDOW), ("rp", WINDOW), ("agg", WINDOW), ("hn", WINDOW),
             ("nst", WINDOW), ("nsw", WINDOW), ("xt", GLANCE), ("kq", GLANCE), ("mt", GRAM)]
MID_ORDER = [("op", SETTLE), ("h2n", SETTLE), ("n2st", SETTLE), ("gate", SETTLE), ("gaten", SETTLE)]

CONSTS = {}
_at = 0
for _name, _width in (("ident", 128), ("band", 256), ("spread", 512), ("tmap", 64), ("lower", 64), ("rankmax", 8),
                      ("vplace", WIN * 32)):
    CONSTS[_name] = (_at, _at + _width)
    _at += _width
CONST_COLS = _at


class Turn:

    def __init__(self, c, j=None):
        self.c, self.j = c, j

    def ago(self, n):
        return Turn(self.c - n, self.j)

    def value(self, per, plus):
        if self.j is None:
            return per * self.c + plus
        return self.j * (2 * per) + (per * self.c + plus)

    def pair(self, stage):
        return Turn(self.c - LAG[stage], self.j)

    def active(self, stage):
        return self.j is not None or 0 <= self.c - LAG[stage] < PAIRS

    @property
    def buf(self):
        return self.c % 2

    def rounds(self, per, plus):
        if self.j is None:
            return per * (self.c // 2) + plus
        return self.j * per + (per * (self.c // 2) + plus)


class Ring:

    def __init__(self, nc, ctx, name, order, slots, banks):
        self.order, self.slots, self.banks = order, slots, banks
        self.filled = [ctx.enter_context(nc.semaphore(f"{name}_filled{n}")) for n in range(slots)]
        self.drained = [ctx.enter_context(nc.semaphore(f"{name}_drained{n}")) for n in range(slots)]

    def use(self, step, turn):
        names = [s for s, _ in self.order]
        if turn.j is None:
            n = sum(Turn(c).active(stage) for c in range(turn.c) for _, stage in self.order)
            n += sum(turn.active(stage) for _, stage in self.order[:names.index(step)])
            return n % self.slots, n // self.slots
        start = sum(Turn(c).active(stage) for c in range(STEADY) for _, stage in self.order)
        n = start + len(names) * (turn.c - STEADY) + names.index(step)
        return n % self.slots, turn.j * (2 * len(names) // self.slots) + n // self.slots


def hold(eng, sem, value):
    if not isinstance(value, int) or value > 0:
        eng.wait_ge(sem, value)


def hi_half(ap):
    return ap.bitcast(BF16).rearrange("p (n two) -> p n two", two=2)[:, :, 1]


def audio_tower(nc, io):
    ctx = ExitStack()
    with ctx:
        def sb(name, shape, dt=F32):
            return ctx.enter_context(nc.sbuf_tensor(name, shape, dt))

        def sem(name):
            return ctx.enter_context(nc.semaphore(name))

        const = sb("const", [128, CONST_COLS])
        key_w = sb("key_w", [128, 128])
        qry_w = sb("qry_w", [128, 128])
        tok_v = sb("tok_v", [128, 1])
        tok_b = sb("tok_b", [128, 1])
        vplace = sb("vplace", [128, WIN, 32])
        a_hi = sb("a_hi", [128, HEADS * C], F32R)
        a_lo = sb("a_lo", [128, HEADS * C], F32R)
        o_w = sb("o_w", [128, HP, C])
        o_bias = sb("o_bias", [128, 1])
        g_w = sb("g_w", [128, 128])
        g_whi = sb("g_whi", [128, 128], F32R)
        g_wlo = sb("g_wlo", [128, 128], F32R)
        g_b = sb("g_b", [128, 1])
        w1_hi = sb("w1_hi", [128, EXPERTS * HID], F32R)
        w1_lo = sb("w1_lo", [128, EXPERTS * HID], F32R)
        b1 = sb("b1", [128, 2 * EXPERTS])
        w2 = sb("w2", [128, 2 * EXPERTS, C])
        b2 = sb("b2", [128, EP])

        xin = sb("xin", [128, 2, 2, 2, C])
        xt = sb("xt", [128, 264])
        kq = sb("kq", [128, 2, 264])
        tanh = sb("tanh", [128, 2, WIN, PADDED])
        sc = sb("sc", [128, 128])
        smax = sb("smax", [QUARTER, 8])
        sexp = sb("sexp", [QUARTER, 8, WIN])
        ssum = sb("ssum", [QUARTER, 8])
        srec = sb("srec", [QUARTER, 8])
        sn = sb("sn", [128, 4, 32])
        wt = sb("wt", [32, PADDED])
        band = sb("band", [128, 2, 2, 128])
        ht = sb("ht", [128, 2, TOKENS])
        stat = sb("stat", [HALF, 2, 8, 4])
        cen = sb("cen", [HALF, 2, 4, C])
        sqr = sb("sqr", [HALF, 2, 4, C])
        nn = sb("nn", [HALF, 2, 4, C])
        nhl = sb("nhl", [HALF, 4, 3 * C], F32R)
        nst = sb("nst", [128, 2, PAIR], F32R)
        nsw = sb("nsw", [128, 2, PAIR], F32R)
        g_hi = sb("g_hi", [128, 2, 2 * HP * TOKENS], F32R)
        g_lo = sb("g_lo", [128, 2, 2 * HP * TOKENS], F32R)
        mx = sb("mx", [128, 2, 2, 2, HP])
        mneg = sb("mneg", [16, TOKENS], F32R)
        prob = sb("prob", [128, 2, 2, 2, HP * TOKENS])
        ut = sb("ut", [128, 2, HP, TOKENS])
        rden = sb("rden", [HALF, 2 * HEADS])
        room = sb("room", [HALF, 4, 8, C])
        un = room[:, :, :, :].rearrange("p (b k) h c -> p b k (h c)", b=2)
        yw = room
        utn = sb("utn", [128, HP, PAIR])
        h2t = sb("h2t", [128, TOKENS])
        h2 = sb("h2", [HALF, 2, 4, C])
        n2 = sb("n2", [HALF, 4, C])
        n2hl = sb("n2hl", [HALF, 4, 2 * C], F32R)
        n2st = sb("n2st", [128, 2, PAIR], F32R)
        gt = sb("gt", [128, PAIR])
        lg = sb("lg", [HALF, 4, EXPERTS])
        gmax = sb("gmax", [HALF, 4])
        gexp = sb("gexp", [HALF, 4, EXPERTS])
        beats = sb("beats", [HALF, 4, EXPERTS, EXPERTS])
        duel = sb("duel", [HALF, 4, EXPERTS, EXPERTS])
        rank = sb("rank", [HALF, 4, EXPERTS])
        comb = sb("comb", [HALF, 2, 4, EXPERTS])
        hid = sb("hid", [128, 4, 2, PAIR])
        yt = sb("yt", [128, EP, PAIR])
        res = sb("res", [HALF, 2, 4, C])

        psum = ctx.enter_context(nc.psum_tensor("psum", [128, 8, 512], F32))
        big = Ring(nc, ctx, "big", BIG_ORDER, 2, 2)
        sums = Ring(nc, ctx, "sums", SUM_ORDER, 2, 1)
        tok = Ring(nc, ctx, "tok", TOK_ORDER, 1, 1)
        mid = Ring(nc, ctx, "mid", MID_ORDER, 1, 1)

        def big_ps(slot):
            return psum[:, 2 * slot:2 * slot + 2, :]

        def sum_ps(slot):
            return psum[:, 4 + slot, :]

        tok_ps, mid_ps = psum[:, 6, :], psum[:, 7, :]

        def cst(name, rows=128):
            a, b = CONSTS[name]
            return const[0:rows, a:b]

        ident = cst("ident")
        wq_in = prob[0:64, 0, 0, 0, 0:512]
        wk_in = prob[0:64, 0, 0, 1, 0:512]
        wv_in = prob[0:64, 0, 1, 0, 0:512]
        wo_in = prob[:, 0, 1, 1, 0:HP * C].rearrange("p (h c) -> p h c", h=HP)
        a_all = ut[:, 0, :, :].rearrange("p h s -> p (h s)")[:, 0:HEADS * C]
        yt_flat = yt[:, :, :].rearrange("p e n -> p (e n)")
        wq_map = yt_flat[:, 0:2 * HP * C].rearrange("p (h k c) -> p h k c", h=HP, k=2)
        wkv_map = yt_flat[:, 2 * HP * C:4 * HP * C].rearrange("p (k h c) -> p k h c", k=2, h=HP)
        w1_in = hid[:, 0:3, :, :].rearrange("p a b n -> p (a b n)")[:, 0:EXPERTS * HID]

        zeroed = sem("zeroed")
        loaded = sem("loaded")
        w_mapped_pe = sem("w_mapped_pe")
        w_mapped = sem("w_mapped")
        x_loaded = [sem("x_loaded0"), sem("x_loaded1")]
        t_summed = sem("t_summed")
        tanh_done = sem("tanh_done")
        s_shifted = sem("s_shifted")
        s_exped = sem("s_exped")
        s_normed = sem("s_normed")
        n_split = sem("n_split")
        g_hi_done = sem("g_hi_done")
        m_stored = [sem("m_stored0"), sem("m_stored1")]
        h2_ready = sem("h2_ready")
        n2_split = sem("n2_split")
        gate_shifted = sem("gate_shifted")
        gate_exped = sem("gate_exped")
        comb_ready = sem("comb_ready")
        y_summed = sem("y_summed")
        out_ready = sem("out_ready")
        out_stored = [sem("out_stored0"), sem("out_stored1")]
        dve_step = sem("dve_step")

        x_v = io["x"].rearrange("(j u b) (lt p) c -> j u p lt b c", u=2, b=2, p=128)
        out_v = io["out"].rearrange("(j u b) (half r) c -> j u r half b c", u=2, b=2, r=HALF)

        block = ctx.enter_context(nc.Block())
        N_LOADS = 23

        def turns(eng, run):
            for c in range(LOOP_FROM):
                run(Turn(c))
            with eng.Fori(LOOP_FROM // 2, LOOP_TO // 2) as j:
                run(Turn(0, j))
                run(Turn(1, j))
            for c in range(LOOP_TO, TURNS):
                run(Turn(c))

        @block.sync
        def _(sp):
            loads = [(const[:, :], io["const"]), (tok_v[0:64, :], io["v"]), (tok_v[64:128, :], io["v"]),
                     (tok_b[0:64, :], io["b"]), (tok_b[64:128, :], io["b"]),
                     (wq_in, io["WQ"]), (wk_in, io["WK"]), (wv_in, io["WV"]),
                     (wo_in, io["Wout"].rearrange("(h p) c -> p h c", p=128)),
                     (o_bias[0:64, :], io["bout"]), (o_bias[64:128, :], io["bout"]),
                     (w1_in[0:64, :], io["W1T"]), (w1_in[64:128, :], io["W1T"]), (b1[:, :], io["b1T"]),
                     (w2[:, :, :], io["W2T"]), (b2[:, :], io["b2T"])]
            for to, of in loads:
                sp.dma_start(to, of).then_inc(loaded, 16)
            sp.wait_ge(zeroed, 1)
            for w, name in ((key_w, "W_key"), (qry_w, "W_qry")):
                for b in range(2):
                    sp.dma_start(w[64 * b:64 * b + 64, 64 * b:64 * b + 64], io[name]).then_inc(loaded, 16)
            for to, of in ((g_w[0:64, 0:EXPERTS], io["WgT"]), (g_w[64:128, 0:EXPERTS], io["WgT"]),
                           (g_b[0:EXPERTS, :], io["bg"])):
                sp.dma_start(to, of).then_inc(loaded, 16)
            assert len(loads) + 4 + 3 == N_LOADS

            def dram(view, turn):
                if turn.j is None:
                    return view[turn.c // 2:turn.c // 2 + 1, turn.buf]
                return view[bass.ds(turn.j + turn.c // 2, 1), turn.buf]

            def run(turn):
                if turn.active(GLANCE):
                    p = turn.pair(GLANCE)
                    if turn.j is not None or p.c >= 2:
                        sp.wait_ge(tok.filled[0], tok.use("agg", turn.ago(1))[1] + 1)
                    for b in range(2):
                        sp.dma_start(xin[:, p.buf, :, b, :],
                                     dram(x_v, p)[:, :, :, b, :].rearrange("a p l c -> p (a l) c")
                                     ).then_inc(x_loaded[p.buf], 16)
                if turn.active(MIX):
                    p = turn.pair(MIX)
                    sp.wait_ge(out_ready, p.value(1, 1))
                    for b in range(2):
                        sp.dma_start(dram(out_v, p)[:, :, :, b, :].rearrange("a r h c -> r (a h) c"),
                                     res[:, p.buf, :, :].rearrange("r (h b) c -> r h b c", b=2)[:, :, b, :]
                                     ).then_inc(out_stored[p.buf], 16)
                if turn.active(GRAM):
                    p = turn.pair(GRAM)
                    slot, n = tok.use("mt", turn)
                    sp.wait_ge(tok.drained[slot], n + 1)
                    for par in range(2):
                        sp.dma_start(g_hi[64 * par + 63:64 * par + 64, p.buf, :].bitcast(F32).rearrange("o (g s) -> o g s", g=8),
                                     mneg[8 * par:8 * par + 8, :].bitcast(F32)).then_inc(m_stored[p.buf], 16)

            turns(sp, run)
            for n in range(2):
                sp.wait_ge(out_stored[n], 32 * (PAIRS // 2))

        @block.gpsimd
        def _(pool):
            def run(turn):
                if turn.active(MIX):
                    p = turn.pair(MIX)
                    for half in range(2):
                        slot, n = big.use(f"yn{half}", turn)
                        pool.wait_ge(big.drained[slot], n + 1)
                        q = yw[:, 2 * half:2 * half + 2]
                        step = p.value(8, 4 * half)
                        for i, width in enumerate((4, 2, 1)):
                            nc.gpsimd.tensor_tensor(q[:, :, 0:width, :], q[:, :, 0:width, :],
                                                    q[:, :, width:2 * width, :], ALU.add).then_inc(y_summed, 1)
                            pool.wait_ge(y_summed, step + i + 1)
                        if half == 0:
                            hold(pool, out_stored[p.buf], p.rounds(32, 0))
                        last = nc.gpsimd.tensor_tensor(res[:, p.buf, 2 * half:2 * half + 2, :], q[:, :, 0, :],
                                                       h2[:, p.buf, 2 * half:2 * half + 2, :], ALU.add)
                        if half == 0:
                            last.then_inc(y_summed, 1)
                        else:
                            last.then_inc(out_ready, 1)
                            pool.wait_ge(out_ready, p.value(1, 1))
                            pool.sem_inc(y_summed, 1)
                if turn.active(GLANCE):
                    p = turn.pair(GLANCE)
                    slot, n = tok.use("kq", turn)
                    pool.wait_ge(tok.drained[slot], n + 1)
                    if turn.j is not None or p.c >= 2:
                        pool.wait_ge(tok.filled[0], tok.use("sc", turn.ago(1))[1] + 1)
                    rows = PADDED // WIN
                    q = kq[:, 1, 0:PADDED].rearrange("p (a e) -> p a e", e=WIN)
                    k = kq[:, 0, 0:PADDED + WIN].rearrange("p (a e) -> p a e", e=WIN)
                    for r in range(WIN):
                        t = tanh[:, p.buf, r, :].rearrange("p (a e) -> p a e", e=WIN)
                        last = nc.gpsimd.tensor_tensor(t[:, :, 0:r + 1], q[:, :, 0:r + 1],
                                                       k[:, 0:rows, r:r + 1].broadcast_to([128, rows, r + 1]),
                                                       ALU.add)
                        if r < WIN - 1:
                            nc.gpsimd.tensor_tensor(t[:, :, r + 1:WIN], q[:, :, r + 1:WIN],
                                                    k[:, 1:rows + 1, r:r + 1].broadcast_to([128, rows, WIN - 1 - r]),
                                                    ALU.add)
                    last.then_inc(t_summed, 1)

            turns(pool, run)

        @block.scalar
        def _(act):
            act.wait_ge(loaded, 16 * N_LOADS)

            def relu(turn, e):
                slot, n = big.use(f"l1_{e}", turn)
                if e >= 4:
                    if e % 2 == 0:
                        s, m = sums.use(f"l2_{(e - 4) // 2}", turn)
                        act.wait_ge(sums.filled[s], m + 1)
                elif e % 2 == 0 and turn.pair(MIX).active(GLANCE) and (turn.j is not None or turn.pair(MIX).c >= 1):
                    s, m = sums.use(f"l2_{2 + e // 2}", turn.ago(1))
                    act.wait_ge(sums.filled[s], m + 1)
                act.wait_ge(big.filled[slot], n + 1)
                for c in range(2):
                    last = nc.scalar.activation(hid[:, e % 4, c, :], big_ps(slot)[:, c, 0:PAIR], ACT.Relu,
                                                bias=b1[:, 2 * e + c:2 * e + c + 1])
                last.then_inc(big.drained[slot], 1)

            def expert_out(turn, ep):
                slot, n = sums.use(f"l2_{ep}", turn)
                if ep == 0 and (turn.j is not None or turn.pair(MIX).c >= 1):
                    s, m = big.use("yn1", turn.ago(1))
                    act.wait_ge(big.filled[s], m + 1)
                act.wait_ge(sums.filled[slot], n + 1)
                nc.scalar.activation(yt[:, ep, :], sum_ps(slot)[:, 0:PAIR], ACT.Identity,
                                     bias=b2[:, ep:ep + 1]).then_inc(sums.drained[slot], 1)

            def attn_back(turn, g):
                slot, n = big.use(f"ub{g}", turn)
                if g == 0 and (turn.j is not None or turn.pair(SETTLE).c >= 1):
                    act.wait_ge(mid.filled[0], mid.use("op", turn.ago(1))[1] + 1)
                act.wait_ge(big.filled[slot], n + 1)
                nc.scalar.activation(utn[:, 2 * g:2 * g + 2, :], big_ps(slot)[:, :, 0:PAIR], ACT.Copy
                                     ).then_inc(big.drained[slot], 1)

            def scores_exp(turn, i):
                p = turn.pair(ATTEND)
                b, tt, par = i // 4, i // 2 % 2, i % 2
                slot, n = big.use(f"s{i}", turn)
                if i % 4 == 0 and (turn.j is not None or p.c >= 1):
                    s, m = sums.use(f"av{2 * b + 1}", turn.ago(1))
                    act.wait_ge(sums.filled[s], m + 1)
                act.wait_ge(big.filled[slot], n + 1)
                nc.scalar.activation(prob[0:HALF, b, tt, par, :].rearrange("p (k n) -> p k n", k=2),
                                     big_ps(slot)[0:HALF, :, 0:PAIR], ACT.Exp).then_inc(big.drained[slot], 1)

            def attn_sums(turn, i):
                slot, n = sums.use(f"av{i}", turn)
                if i == 0 and (turn.j is not None or turn.pair(ATTEND).c >= 1):
                    s, m = big.use("un1", turn)
                    act.wait_ge(big.filled[s], m + 1)
                act.wait_ge(sums.filled[slot], n + 1)
                nc.scalar.activation(ut[:, i // 2, 2 * (i % 2):2 * (i % 2) + 2, :],
                                     sum_ps(slot)[:, 0:PAIR].rearrange("p (k n) -> p k n", k=2), ACT.Copy
                                     ).then_inc(sums.drained[slot], 1)

            def run(turn):
                win, glance, gram = turn.active(WINDOW), turn.active(GLANCE), turn.active(GRAM)
                attend, settle, mix = turn.active(ATTEND), turn.active(SETTLE), turn.active(MIX)
                if mix:
                    relu(turn, 0)
                if win:
                    p = turn.pair(WINDOW)
                    act.wait_ge(s_shifted, p.value(1, 1))
                    nc.scalar.activation(sexp[:, :, :], sexp[:, :, :], ACT.Exp).then_inc(s_exped, 1)
                if mix:
                    relu(turn, 1)
                    relu(turn, 2)
                if settle:
                    attn_back(turn, 0)
                if mix:
                    relu(turn, 3)
                    expert_out(turn, 0)
                if settle:
                    attn_back(turn, 1)
                if mix:
                    relu(turn, 4)
                    expert_out(turn, 1)
                    relu(turn, 5)
                if settle:
                    p = turn.pair(SETTLE)
                    slot, n = mid.use("h2n", turn)
                    hold(act, out_ready, p.value(1, -1))
                    act.wait_ge(mid.filled[slot], n + 1)
                    nc.scalar.activation(h2[:, p.buf, :, :].rearrange("p q c -> p (q c)"),
                                         mid_ps[0:HALF, 0:4 * C], ACT.Copy).then_inc(mid.drained[slot], 1)
                if mix:
                    relu(turn, 6)
                    expert_out(turn, 2)
                    relu(turn, 7)
                    expert_out(turn, 3)
                if settle:
                    slot, n = mid.use("n2st", turn)
                    if turn.j is not None or p.c >= 2:
                        s, m = big.use("l1_7", turn.ago(1))
                        act.wait_ge(big.filled[s], m + 1)
                    act.wait_ge(mid.filled[slot], n + 1)
                    nc.scalar.activation(n2st[:, p.buf, :], mid_ps[:, 0:PAIR], ACT.Copy
                                         ).then_inc(mid.drained[slot], 1)
                if win:
                    p = turn.pair(WINDOW)
                    if turn.j is not None or p.c >= 2:
                        s, m = big.use("s7", turn.ago(1))
                        act.wait_ge(big.filled[s], m + 1)
                    for step, to in (("nst", nst), ("nsw", nsw)):
                        slot, n = tok.use(step, turn)
                        act.wait_ge(tok.filled[slot], n + 1)
                        nc.scalar.activation(to[:, p.buf, :], tok_ps[:, 0:PAIR], ACT.Copy
                                             ).then_inc(tok.drained[slot], 1)
                if settle:
                    slot, n = mid.use("gate", turn)
                    act.wait_ge(mid.filled[slot], n + 1)
                    nc.scalar.activation(gt[:, :], mid_ps[:, 0:PAIR], ACT.Identity, bias=g_b[:, :]
                                         ).then_inc(mid.drained[slot], 1)
                    p = turn.pair(SETTLE)
                if gram:
                    p = turn.pair(GRAM)
                    for g in range(2):
                        slot, n = big.use(f"g{g}", turn)
                        if g == 0 and (turn.j is not None or p.c >= 2):
                            s, m = big.use("s7", turn.ago(1))
                            act.wait_ge(big.filled[s], m + 1)
                        act.wait_ge(big.filled[slot], n + 1)
                        for k in range(2):
                            nc.scalar.activation(
                                g_hi[:, p.buf, :].rearrange("p (b h s) -> p b h s", b=2, h=HP)[:, :, 2 * g + k, :],
                                big_ps(slot)[:, k, 0:PAIR].rearrange("p (b s) -> p b s", b=2), ACT.Copy
                            ).then_inc(g_hi_done, 1)
                if settle:
                    p = turn.pair(SETTLE)
                    act.wait_ge(gate_shifted, p.value(1, 1))
                    nc.scalar.activation(gexp[:, :, :], gexp[:, :, :], ACT.Exp).then_inc(gate_exped, 1)
                for i in range(8):
                    if attend:
                        scores_exp(turn, i)
                        if i == 5:
                            attn_sums(turn, 0)
                        if i == 6:
                            attn_sums(turn, 1)
                    if i == 5 and glance:
                        p = turn.pair(GLANCE)
                        act.wait_ge(t_summed, p.value(1, 1))
                        t = tanh[:, p.buf, :, :].rearrange("p r w -> p (r w)")
                        nc.scalar.activation(t, t, ACT.Tanh, bias=tok_b[:, :]).then_inc(tanh_done, 1)
                if attend:
                    attn_sums(turn, 2)
                    attn_sums(turn, 3)
                if gram:
                    p = turn.pair(GRAM)
                    slot, n = tok.use("mt", turn)
                    hold(act, m_stored[(p.c + 1) % 2], p.ago(1).rounds(32, 32) if p.j is not None or p.c else 0)
                    act.wait_ge(tok.filled[slot], n + 1)
                    nc.scalar.activation(mneg[:, :], tok_ps[0:16, 0:TOKENS], ACT.Copy, scale=-1.0
                                         ).then_inc(tok.drained[slot], 1)

            turns(act, run)

        @block.vector
        def _(dve):
            count = {"base": 0, "n": 0}

            def link(ins):
                count["n"] += 1
                ins.then_inc(dve_step, 1)
                dve.wait_ge(dve_step, count["base"] + count["n"])

            V = nc.vector
            for t in (key_w[:, :], qry_w[:, :], xt[:, :], kq[:, :, :], sc[:, :], sn[:, :, :], g_w[:, :], g_b[:, :]):
                V.memset(t, 0.0)
            V.memset(nn[:, :, :, C - 1:C], 1.0).then_inc(zeroed, 1)
            dve.wait_ge(loaded, 16 * N_LOADS)
            V.tensor_scalar(vplace[:, :, :].rearrange("p r m -> p (r m)"), cst("vplace"), tok_v[:, 0:1], None,
                            ALU.mult)
            for hi, lo, of in ((w1_hi, w1_lo, w1_in), (g_whi, g_wlo, g_w[:, :])):
                link(V.tensor_copy(hi[:, :], of))
                link(V.tensor_tensor(lo[:, :], of, hi[:, :], ALU.subtract))
            dve.wait_ge(w_mapped_pe, 1)
            V.tensor_copy(wq_map[:, :, :, :], psum[:, 0, 0:HP * C].rearrange("p (h o c) -> p h o c", h=HP, o=1)
                          .broadcast_to([128, HP, 2, C]))
            V.tensor_copy(wkv_map[:, :, :, :].rearrange("p k h c -> p (k h c)"), psum[:, 1, 0:2 * HP * C]
                          ).then_inc(w_mapped, 1)
            dve.wait_ge(w_mapped_pe, 2)
            for par in range(2):
                V.tensor_scalar(a_all.rearrange("p (h k c) -> p h k c", h=HP, k=2)[:, :, par, :],
                                psum[:, 2 + par, 0:HP * C].rearrange("p (h c) -> p h c", h=HP),
                                ATTN_SCALE, None, ALU.mult)
                last = V.tensor_copy(o_w[64 * par:64 * par + 64, :, :].rearrange("p h c -> p (h c)"),
                                     psum[64 * par:64 * par + 64, 4 + par, 0:HP * C])
            link(last)
            link(V.tensor_copy(a_hi[:, :], a_all))
            V.tensor_tensor(a_lo[:, :], a_all, a_hi[:, :], ALU.subtract).then_inc(w_mapped, 1)

            def layer_norm(which, src, to, width, freed=None):
                s = stat[:, which]
                c, q = cen[:, which], sqr[:, which]
                link(V.tensor_reduce(s[:, 0, :], src, AX.X, ALU.add))
                link(V.tensor_scalar(s[:, 1, :], s[:, 0, :], -1.0 / C, None, ALU.mult))
                ins = V.tensor_tensor(c, src, s[:, 1, :].rearrange("p (q o) -> p q o", o=1)
                                      .broadcast_to([HALF, 4, C]), ALU.add)
                if freed is None:
                    link(ins)
                else:
                    ins.then_inc(freed[0], 1)
                    dve.wait_ge(freed[0], freed[1])
                link(V.tensor_tensor(q, c, c, ALU.mult))
                link(V.tensor_reduce(s[:, 2, :], q, AX.X, ALU.add))
                link(V.tensor_scalar(s[:, 2, :], s[:, 2, :], 1.0 / C, EPS, ALU.mult, ALU.add))
                v, y, t = s[:, 2, :], s[:, 3, :], s[:, 4, :]
                link(V.tensor_single_scalar(y.bitcast(I32), v.bitcast(I32), 1, ALU.logical_shift_right))
                link(V.tensor_scalar(y.bitcast(I32), y.bitcast(I32), -1.0, float(RSQRT_GUESS), ALU.mult, ALU.add))
                for _ in range(4):
                    link(V.scalar_tensor_tensor(t, y, -0.5, y, ALU.mult, ALU.mult))
                    link(V.tensor_tensor(t, t, v, ALU.mult))
                    link(V.scalar_tensor_tensor(y, t, 1.5, y, ALU.add, ALU.mult))
                link(V.tensor_tensor(to[:, :, 0:width], c[:, :, 0:width],
                                     y.rearrange("p (q o) -> p q o", o=1).broadcast_to([HALF, 4, width]), ALU.mult))

            def normalise(turn, b):
                slot, n = big.use(f"un{b}", turn)
                dve.wait_ge(big.filled[slot], n + 1)
                u = big_ps(slot)[0:HALF].rearrange("p k (h c) -> p (k h) c", c=C)
                link(V.reciprocal(rden[:, :], u[:, :, C - 1]))
                if b == 0:
                    hold(dve, out_ready, turn.pair(MIX).value(1, 0))
                V.tensor_tensor(un[:, b, :, :].rearrange("p k (h c) -> p (k h) c", c=C), u,
                                rden[:, :].rearrange("p (h o) -> p h o", o=1).broadcast_to([HALF, 16, C]), ALU.mult
                                ).then_inc(big.drained[slot], 1)

            def weigh(turn, half):
                p = turn.pair(MIX)
                slot, n = big.use(f"yn{half}", turn)
                if half == 0 and turn.active(SETTLE):
                    s, m = big.use("ub1", turn)
                    dve.wait_ge(big.filled[s], m + 1)
                elif half == 0:
                    hold(dve, out_ready, p.value(1, 0))
                dve.wait_ge(comb_ready, p.value(1, 1))
                dve.wait_ge(big.filled[slot], n + 1)
                V.tensor_tensor(yw[:, 2 * half:2 * half + 2].rearrange("p q e c -> p (q e) c"),
                                big_ps(slot)[0:HALF].rearrange("p k (e c) -> p (k e) c", c=C),
                                comb[:, p.buf, 2 * half:2 * half + 2, :].rearrange("p q (e o) -> p (q e) o", o=1)
                                .broadcast_to([HALF, 16, C]), ALU.mult).then_inc(big.drained[slot], 1)

            def row_max(turn, i):
                b, st, par = i // 4, i // 2 % 2, i % 2
                slot, n = big.use(f"mx{i}", turn)
                if i == 0 and (turn.j is not None or turn.pair(GRAM).c >= 1):
                    dve.wait_ge(tok.filled[0], tok.use("mt", turn.ago(1))[1] + 1)
                dve.wait_ge(big.filled[slot], n + 1)
                V.tensor_reduce(mx[:, st, par, b, :].rearrange("p (k h) -> p k h", k=2),
                                big_ps(slot)[:, :, 0:PAIR].rearrange("p k (h s) -> p k h s", h=2),
                                AX.X, ALU.max).then_inc(big.drained[slot], 1)

            def tok_copy(turn, step, to, of):
                slot, n = tok.use(step, turn)
                dve.wait_ge(tok.filled[slot], n + 1)
                V.tensor_copy(to, of).then_inc(tok.drained[slot], 1)

            def run(turn):
                win, glance, gram = turn.active(WINDOW), turn.active(GLANCE), turn.active(GRAM)
                attend, settle, mix = turn.active(ATTEND), turn.active(SETTLE), turn.active(MIX)
                if settle:
                    normalise(turn, 0)
                if win:
                    p = turn.pair(WINDOW)
                    tok_copy(turn, "sc", sc[:, 0:QUARTER], tok_ps[:, 0:QUARTER])
                    slot, n = tok.use("scn", turn)
                    dve.wait_ge(tok.filled[slot], n + 1)
                    s = (tok_ps[0:QUARTER, 0:128].rearrange("p (j m) -> p j m", m=32)[:, :, 0:2 * WIN]
                         .rearrange("p j (b r) -> p j b r", b=2))
                    link(V.tensor_reduce(smax[:, :].rearrange("p (j b) -> p j b", b=2), s, AX.X, ALU.max))
                    V.tensor_tensor(sexp[:, :, :].rearrange("p (j b) r -> p j b r", b=2), s,
                                    smax[:, :].rearrange("p (j b o) -> p j b o", b=2, o=1)
                                    .broadcast_to([QUARTER, 4, 2, WIN]), ALU.subtract).then_inc(tok.drained[slot], 1)
                    dve.wait_ge(tok.drained[slot], n + 1)
                    dve.sem_inc(s_shifted, 1)
                if settle:
                    normalise(turn, 1)
                if win:
                    dve.wait_ge(s_exped, p.value(1, 1))
                    link(V.tensor_reduce(ssum[:, :], sexp[:, :, :], AX.X, ALU.add))
                    link(V.reciprocal(srec[:, :], ssum[:, :]))
                    V.tensor_tensor(sn[0:QUARTER, :, 0:2 * WIN].rearrange("p j (b r) -> p j b r", b=2),
                                    sexp[:, :, :].rearrange("p (j b) r -> p j b r", b=2),
                                    srec[:, :].rearrange("p (j b o) -> p j b o", b=2, o=1)
                                    .broadcast_to([QUARTER, 4, 2, WIN]), ALU.mult).then_inc(s_normed, 1)
                    tok_copy(turn, "et", wt[:, :], tok_ps[0:32, 0:PADDED])
                    slot, n = tok.use("rp", turn)
                    dve.wait_ge(tok.filled[slot], n + 1)
                    V.tensor_tensor(band[:, :, :, :].rearrange("p b t w -> p b (t w)"),
                                    tok_ps[:, 0:512].rearrange("p (b w) -> p b w", b=2),
                                    cst("band").rearrange("p (o w) -> p o w", o=1).broadcast_to([128, 2, 256]),
                                    ALU.mult).then_inc(tok.drained[slot], 1)
                if settle:
                    p = turn.pair(SETTLE)
                    slot, n = mid.use("op", turn)
                    dve.wait_ge(mid.filled[slot], n + 1)
                    V.scalar_tensor_tensor(h2t[:, :], mid_ps[:, 0:TOKENS], o_bias[:, 0:1], ht[:, p.buf, :],
                                           ALU.add, ALU.add).then_inc(mid.drained[slot], 1)
                if win:
                    p = turn.pair(WINDOW)
                    if settle:
                        slot, n = mid.use("op", turn)
                        dve.wait_ge(mid.drained[slot], n + 1)
                    tok_copy(turn, "agg", ht[:, p.buf, :], tok_ps[:, 0:TOKENS])
                if settle:
                    p = turn.pair(SETTLE)
                    slot, n = mid.use("h2n", turn)
                    dve.wait_ge(mid.drained[slot], n + 1)
                    layer_norm(1, h2[:, p.buf], n2, C)
                    if turn.j is not None or p.c >= 1:
                        dve.wait_ge(mid.filled[0], mid.use("n2st", turn.ago(1))[1] + 1)
                    link(V.tensor_copy(n2hl[:, :, 0:C], n2[:, :, :]))
                    V.tensor_tensor(n2hl[:, :, C:2 * C], n2[:, :, :], n2hl[:, :, 0:C], ALU.subtract
                                    ).then_inc(n2_split, 1)
                if win:
                    p = turn.pair(WINDOW)
                    slot, n = tok.use("hn", turn)
                    dve.wait_ge(tok.filled[slot], n + 1)
                    if turn.j is not None or p.c >= 2:
                        s, m = sums.use("av3", turn.ago(1))
                        dve.wait_ge(sums.filled[s], m + 1)
                    layer_norm(0, tok_ps[0:HALF, 0:4 * C].rearrange("p (q c) -> p q c", c=C), nn[:, p.buf], C - 1,
                               freed=(tok.drained[slot], n + 1))
                    if turn.j is not None or p.c >= 1:
                        dve.wait_ge(tok.filled[0], tok.use("nsw", turn.ago(1))[1] + 1)
                    for k in (0, 2):
                        link(V.tensor_copy(nhl[:, :, k * C:(k + 1) * C], nn[:, p.buf]))
                    V.tensor_tensor(nhl[:, :, C:2 * C], nn[:, p.buf], nhl[:, :, 0:C], ALU.subtract
                                    ).then_inc(n_split, 1)
                if mix:
                    weigh(turn, 0)
                    weigh(turn, 1)
                if settle:
                    p = turn.pair(SETTLE)
                    slot, n = mid.use("gaten", turn)
                    dve.wait_ge(mid.filled[slot], n + 1)
                    V.tensor_copy(lg[:, :, :], mid_ps[0:HALF, :].rearrange("p (q e) -> p q e", q=4)[:, :, 0:EXPERTS]
                                  ).then_inc(mid.drained[slot], 1)
                    dve.wait_ge(mid.drained[slot], n + 1)
                    link(V.tensor_reduce(gmax[:, :], lg[:, :, :], AX.X, ALU.max))
                    V.tensor_tensor(gexp[:, :, :], lg[:, :, :], gmax[:, :].rearrange("p (q o) -> p q o", o=1)
                                    .broadcast_to([HALF, 4, EXPERTS]), ALU.subtract).then_inc(gate_shifted, 1)
                    every = [HALF, 4, EXPERTS, EXPERTS]
                    link(V.tensor_tensor(beats[:, :, :, :],
                                         lg[:, :, :].rearrange("p q (o e) -> p q o e", o=1).broadcast_to(every),
                                         lg[:, :, :].rearrange("p q (e o) -> p q e o", o=1).broadcast_to(every),
                                         ALU.is_ge))
                    link(V.tensor_tensor(duel[:, :, :, :].rearrange("p q e f -> p q (e f)"),
                                         beats[:, :, :, :].rearrange("p q e f -> p q (e f)"),
                                         cst("lower", HALF).rearrange("p (o e) -> p o e", o=1)
                                         .broadcast_to([HALF, 4, EXPERTS * EXPERTS]), ALU.mult))
                    link(V.tensor_tensor(beats[:, :, :, :], duel[:, :, :, :],
                                         duel[:, :, :, :].rearrange("p q e f -> p q f e"), ALU.subtract))
                    link(V.tensor_reduce(rank[:, :, :], beats[:, :, :, :], AX.X, ALU.add))
                    link(V.tensor_tensor(rank[:, :, :], rank[:, :, :],
                                         cst("rankmax", HALF).rearrange("p (o e) -> p o e", o=1)
                                         .broadcast_to([HALF, 4, EXPERTS]), ALU.is_lt))
                    dve.wait_ge(gate_exped, p.value(1, 1))
                    link(V.tensor_tensor(rank[:, :, :], rank[:, :, :], gexp[:, :, :], ALU.mult))
                    link(V.tensor_reduce(gmax[:, :], rank[:, :, :], AX.X, ALU.add))
                    link(V.reciprocal(gmax[:, :], gmax[:, :]))
                    V.tensor_tensor(comb[:, p.buf], rank[:, :, :], gmax[:, :].rearrange("p (q o) -> p q o", o=1)
                                    .broadcast_to([HALF, 4, EXPERTS]), ALU.mult).then_inc(comb_ready, 1)
                if gram:
                    p = turn.pair(GRAM)
                    for g in range(2):
                        slot, n = big.use(f"g{g}", turn)
                        for k in range(2):
                            at = (g_hi[:, p.buf, :], g_lo[:, p.buf, :])
                            hi, lo = (t.rearrange("p (b h s) -> p b h s", b=2, h=HP)[:, :, 2 * g + k, :] for t in at)
                            dve.wait_ge(g_hi_done, p.value(4, 2 * g + 2))
                            last = V.tensor_tensor(lo, big_ps(slot)[:, k, 0:PAIR].rearrange("p (b s) -> p b s", b=2),
                                                   hi, ALU.subtract)
                        last.then_inc(big.drained[slot], 1)
                if gram:
                    row_max(turn, 0)
                if glance:
                    tok_copy(turn, "xt", xt[:, 0:LENGTH], tok_ps[:, 0:LENGTH])
                if gram:
                    row_max(turn, 1)
                if glance:
                    p = turn.pair(GLANCE)
                    hold(dve, t_summed, p.value(1, 0))
                    tok_copy(turn, "kq", kq[:, :, 0:LENGTH], tok_ps[:, 0:512].rearrange("p (k n) -> p k n", k=2))
                if gram:
                    for i in range(2, 8):
                        row_max(turn, i)

            def counted(turn):
                count["base"], count["n"] = count["base"] + count["n"], 0
                run(turn)

            for c in range(LOOP_FROM):
                counted(Turn(c))
            start, per = count["base"] + count["n"], count["n"]
            with dve.Fori(LOOP_FROM // 2, LOOP_TO // 2) as j:
                for u in range(2):
                    count["base"], count["n"] = j * (2 * per) + (start - LOOP_FROM * per + u * per), 0
                    run(Turn(u, j))
                    assert count["n"] == per
            count["base"], count["n"] = start + (LOOP_TO - LOOP_FROM) * per, 0
            for c in range(LOOP_TO, TURNS):
                counted(Turn(c))

        @block.tensor
        def _(pe):
            mm = nc.tensor.matmul

            pe.wait_ge(zeroed, 1)
            pe.wait_ge(loaded, 16 * N_LOADS)
            for k, w in enumerate((wq_in, wk_in, wv_in)):
                for hp in range(HP):
                    at = hp * C if k == 0 else ((k - 1) * HP + hp) * C
                    last = mm(psum[:, min(k, 1), at:at + C], w[:, 128 * hp:128 * hp + 128], cst("tmap", 64),
                              start=True, stop=True)
            last.then_inc(w_mapped_pe, 1)
            pe.wait_ge(w_mapped, 1)
            for par in range(2):
                r = slice(64 * par, 64 * par + 64)
                for hp in range(HP):
                    at = slice(hp * C, hp * C + C)
                    mm(psum[:, 2 + par, at], wq_map[r, hp].rearrange("p o c -> p (o c)"), wkv_map[r, 0, hp],
                       start=True, stop=True)
                    last = mm(psum[r, 4 + par, at], wkv_map[r, 1, hp], wo_in[r, hp, :], start=True, stop=True)
            last.then_inc(w_mapped_pe, 1)
            pe.wait_ge(w_mapped, 2)

            def flip(out, of, last=None):
                rows = of.shape[0]
                return nc.tensor.transpose(out, of, ident[0:rows, 0:rows])

            def free(ring, step, turn):
                slot, n = ring.use(step, turn)
                hold(pe, ring.drained[slot], n)
                return slot

            def ln_cols(q):
                at = (q % 2) * TOKENS + (q // 2) * HALF
                return slice(at, at + HALF)

            def attn_rows(turn, b):
                if b == 0:
                    for i in (2, 3):
                        s, m = sums.use(f"av{i}", turn.ago(1))
                        pe.wait_ge(sums.drained[s], m + 1)
                slot = free(big, f"un{b}", turn)
                for half in range(2):
                    for hp in range(HP):
                        last = flip(big_ps(slot)[0:HALF, half, 128 * hp:128 * hp + 128],
                                    ut[:, b, hp, half * HALF:(half + 1) * HALF])
                last.then_inc(big.filled[slot], 1)

            def attn_cols(turn, g):
                if g == 0:
                    for b in range(2):
                        s, m = big.use(f"un{b}", turn)
                        pe.wait_ge(big.drained[s], m + 1)
                slot = free(big, f"ub{g}", turn)
                for k in range(2):
                    for b in range(2):
                        for half in range(2):
                            at = b * TOKENS + half * HALF
                            hp = 2 * g + k
                            last = flip(big_ps(slot)[:, k, at:at + HALF], un[:, b, half, 128 * hp:128 * hp + 128])
                last.then_inc(big.filled[slot], 1)

            def layer1(turn, e):
                p = turn.pair(MIX)
                if e == 0:
                    pe.wait_ge(mid.drained[0], mid.use("n2st", turn.ago(1))[1] + 1)
                slot = free(big, f"l1_{e}", turn)
                for c in range(2):
                    at = slice((2 * e + c) * 128, (2 * e + c + 1) * 128)
                    for w in (w1_hi, w1_lo):
                        last = mm(big_ps(slot)[:, c, 0:PAIR], w[:, at], n2st[:, p.buf, :],
                                  start=(w is w1_hi), stop=(w is w1_lo))
                last.then_inc(big.filled[slot], 1)

            def layer2(turn, ep):
                for e in (2 * ep, 2 * ep + 1):
                    s, m = big.use(f"l1_{e}", turn)
                    pe.wait_ge(big.drained[s], m + 1)
                slot = free(sums, f"l2_{ep}", turn)
                for c in range(2):
                    for par in range(2):
                        e = 2 * ep + par
                        last = mm(sum_ps(slot)[64 * par:64 * par + 64, 0:PAIR], w2[:, 2 * e + c, :],
                                  hid[:, e % 4, c, :], start=(c == 0), stop=(c == 1))
                last.then_inc(sums.filled[slot], 1)

            def yn(turn, half):
                if half == 0:
                    for ep in (2, 3):
                        s, m = sums.use(f"l2_{ep}", turn)
                        pe.wait_ge(sums.drained[s], m + 1)
                slot = free(big, f"yn{half}", turn)
                for b in range(2):
                    for ep in range(EP):
                        last = flip(big_ps(slot)[0:HALF, b, 128 * ep:128 * ep + 128], yt[:, ep, ln_cols(2 * half + b)])
                last.then_inc(big.filled[slot], 1)

            def score(turn, i):
                p = turn.pair(ATTEND)
                b, tt, par = i // 4, i // 2 % 2, i % 2
                r = slice(64 * par, 64 * par + 64)
                n_hi, n_lo = (nst, nsw) if par == 0 else (nsw, nst)
                keys = slice(b * TOKENS + tt * HALF, b * TOKENS + (tt + 1) * HALF)
                if i == 0:
                    pe.wait_ge(m_stored[p.buf], p.rounds(32, 32))
                slot = free(big, f"s{i}", turn)
                for k in range(2):
                    q = slice((b * HP + 2 * k) * TOKENS, (b * HP + 2 * k + 2) * TOKENS)
                    for w, g in ((n_hi, g_hi), (n_hi, g_lo), (n_lo, g_hi)):
                        last = mm(big_ps(slot)[0:HALF, k, 0:PAIR], w[r, p.buf, keys], g[r, p.buf, q],
                                  start=(w is n_hi and g is g_hi), stop=(w is n_lo))
                last.then_inc(big.filled[slot], 1)

            def attend_sum(turn, i):
                p = turn.pair(ATTEND)
                b, k = i // 2, i % 2
                if k == 0:
                    for s_i in (4 * b + 2, 4 * b + 3):
                        s, m = big.use(f"s{s_i}", turn)
                        pe.wait_ge(big.drained[s], m + 1)
                slot = free(sums, f"av{i}", turn)
                for tt in range(2):
                    for par in range(2):
                        last = mm(sum_ps(slot)[64 * par:64 * par + 64, 0:PAIR], nn[:, p.buf, 2 * tt + b, :],
                                  prob[0:HALF, b, tt, par, PAIR * k:PAIR * k + PAIR], start=(tt == 0), stop=(tt == 1))
                last.then_inc(sums.filled[slot], 1)

            def row_max(turn, i):
                p = turn.pair(GRAM)
                b, st, par = i // 4, i // 2 % 2, i % 2
                r = slice(64 * par, 64 * par + 64)
                n_hi = nst if par == 0 else nsw
                if i == 0:
                    pe.wait_ge(g_hi_done, p.value(4, 4))
                slot = free(big, f"mx{i}", turn)
                for hp in range(HP):
                    at = (b * HP + hp) * TOKENS + st * (TOKENS - 128)
                    last = mm(big_ps(slot)[:, hp // 2, TOKENS * (hp % 2):TOKENS * (hp % 2) + TOKENS],
                              hi_half(g_hi[r, p.buf, at:at + 128]),
                              hi_half(n_hi[r, p.buf, b * TOKENS:(b + 1) * TOKENS]), start=True, stop=True)
                last.then_inc(big.filled[slot], 1)

            def run(turn):
                win, glance, gram = turn.active(WINDOW), turn.active(GLANCE), turn.active(GRAM)
                attend, settle, mix = turn.active(ATTEND), turn.active(SETTLE), turn.active(MIX)
                wp, gp = turn.pair(WINDOW), turn.pair(GLANCE)
                if settle:
                    attn_rows(turn, 0)
                if win:
                    pe.wait_ge(tanh_done, wp.value(1, 1))
                    free(tok, "sc", turn)
                    for r in range(WIN):
                        for qt in range(4):
                            last = mm(tok_ps[32 * qt:32 * qt + 32, 0:QUARTER], vplace[:, r, :],
                                      tanh[:, wp.buf, r, QUARTER * qt:QUARTER * (qt + 1)],
                                      start=(r == 0), stop=(r == WIN - 1))
                    last.then_inc(tok.filled[0], 1)
                if mix:
                    layer1(turn, 0)
                if win:
                    free(tok, "scn", turn)
                    flip(tok_ps[:, 0:128], sc[:, :]).then_inc(tok.filled[0], 1)
                if settle:
                    attn_rows(turn, 1)
                if mix:
                    layer1(turn, 1)
                    layer1(turn, 2)
                if settle:
                    attn_cols(turn, 0)
                if win:
                    pe.wait_ge(s_normed, wp.value(1, 1))
                    free(tok, "et", turn)
                    for qt in range(4):
                        last = flip(tok_ps[0:32, QUARTER * qt:QUARTER * qt + 128], sn[:, qt, :])
                    last.then_inc(tok.filled[0], 1)
                if mix:
                    layer1(turn, 3)
                    layer2(turn, 0)
                if settle:
                    attn_cols(turn, 1)
                if win:
                    free(tok, "rp", turn)
                    oh = cst("spread", 32).rearrange("p (b t l) -> p b t l", b=2, t=2)
                    for b in range(2):
                        for lt in range(2):
                            w0 = lt * (TOKENS - 128)
                            last = mm(tok_ps[:, (2 * b + lt) * 128:(2 * b + lt + 1) * 128], oh[:, b, lt, :],
                                      wt[:, w0:w0 + 128], start=True, stop=True)
                    last.then_inc(tok.filled[0], 1)
                if mix:
                    layer1(turn, 4)
                    layer2(turn, 1)
                if settle:
                    for g in range(2):
                        s, m = big.use(f"ub{g}", turn)
                        pe.wait_ge(big.drained[s], m + 1)
                    free(mid, "op", turn)
                    for hp in range(HP):
                        for b in range(2):
                            last = mm(mid_ps[64 * b:64 * b + 64, 0:TOKENS], o_w[:, hp, :],
                                      utn[:, hp, b * TOKENS:(b + 1) * TOKENS], start=(hp == 0), stop=(hp == HP - 1))
                    last.then_inc(mid.filled[0], 1)
                if win:
                    free(tok, "agg", turn)
                    for lt in range(2):
                        w0 = lt * (TOKENS - 128)
                        for b in range(2):
                            last = mm(tok_ps[64 * b:64 * b + 64, w0:w0 + 128], xin[:, wp.buf, lt, b, :],
                                      band[:, b, lt, :], start=(lt == 0), stop=(lt == 1), skip_group_check=True)
                    last.then_inc(tok.filled[0], 1)
                if mix:
                    layer1(turn, 5)
                if settle:
                    free(mid, "h2n", turn)
                    for half in range(2):
                        last = flip(mid_ps[0:HALF, 128 * half:128 * half + 128], h2t[:, half * HALF:(half + 1) * HALF])
                    last.then_inc(mid.filled[0], 1)
                if win:
                    free(tok, "hn", turn)
                    for half in range(2):
                        last = flip(tok_ps[0:HALF, 128 * half:128 * half + 128],
                                    ht[:, wp.buf, half * HALF:(half + 1) * HALF])
                    last.then_inc(tok.filled[0], 1)
                if mix:
                    layer1(turn, 6)
                    layer2(turn, 2)
                    layer1(turn, 7)
                    layer2(turn, 3)
                if settle:
                    pe.wait_ge(n2_split, turn.pair(SETTLE).value(1, 1))
                    free(mid, "n2st", turn)
                    for q in range(4):
                        last = flip(mid_ps[:, ln_cols(q)], n2hl[:, q, :].bitcast(F32))
                    last.then_inc(mid.filled[0], 1)
                if win:
                    pe.wait_ge(n_split, wp.value(1, 1))
                    for step, at in (("nst", 0), ("nsw", C)):
                        free(tok, step, turn)
                        for q in range(4):
                            last = flip(tok_ps[:, ln_cols(q)], nhl[:, q, at:at + 128].bitcast(F32))
                        last.then_inc(tok.filled[0], 1)
                if settle:
                    free(mid, "gate", turn)
                    sbuf = turn.pair(SETTLE).buf
                    mm(mid_ps[:, 0:PAIR], g_whi[:, :], n2st[:, sbuf, :], start=True, stop=False)
                    mm(mid_ps[:, 0:PAIR], g_wlo[:, :], n2st[:, sbuf, :], start=False, stop=True
                       ).then_inc(mid.filled[0], 1)
                if mix:
                    yn(turn, 0)
                    yn(turn, 1)
                if settle:
                    free(mid, "gaten", turn)
                    for q in range(4):
                        last = flip(mid_ps[0:HALF, 128 * q:128 * (q + 1)], gt[:, ln_cols(q)])
                    last.then_inc(mid.filled[0], 1)
                if gram:
                    pe.wait_ge(tok.drained[0], tok.use("nsw", turn)[1] + 1)
                    for g in range(2):
                        slot = free(big, f"g{g}", turn)
                        for k in range(2):
                            at = slice((2 * g + k) * 128, (2 * g + k + 1) * 128)
                            for w in (a_hi, a_lo):
                                last = mm(big_ps(slot)[:, k, 0:PAIR], w[:, at], nst[:, turn.pair(GRAM).buf, :],
                                          start=(w is a_hi), stop=(w is a_lo))
                        last.then_inc(big.filled[slot], 1)
                if attend:
                    score(turn, 0)
                    score(turn, 1)
                if glance:
                    pe.wait_ge(x_loaded[gp.buf], gp.rounds(32, 32))
                    free(tok, "xt", turn)
                    for lt in range(2):
                        last = flip(tok_ps[:, 128 * lt:128 * lt + 128],
                                    xin[:, gp.buf, lt, :, :].rearrange("p b c -> p (b c)"))
                    last.then_inc(tok.filled[0], 1)
                if gram:
                    row_max(turn, 0)
                if attend:
                    score(turn, 2)
                if glance:
                    free(tok, "kq", turn)
                    mm(tok_ps[:, 0:LENGTH], key_w[:, :], xt[:, 0:LENGTH], start=True, stop=True)
                    mm(tok_ps[:, LENGTH:2 * LENGTH], qry_w[:, :], xt[:, WIN // 2:WIN // 2 + LENGTH],
                       start=True, stop=True).then_inc(tok.filled[0], 1)
                for i in range(1, 8):
                    if gram:
                        row_max(turn, i)
                    if attend:
                        if i + 2 < 8:
                            score(turn, i + 2)
                        if i in (3, 4):
                            attend_sum(turn, i - 3)
                if attend:
                    attend_sum(turn, 2)
                    attend_sum(turn, 3)
                if gram:
                    s, m = big.use("mx7", turn)
                    pe.wait_ge(big.drained[s], m + 1)
                    free(tok, "mt", turn)
                    for st in range(2):
                        at = st * (TOKENS - 128)
                        last = flip(tok_ps[0:16, at:at + 128], mx[:, st].rearrange("p k b h -> p (k b h)"))
                    last.then_inc(tok.filled[0], 1)

            turns(pe, run)


def constants():
    out = np.zeros((128, CONST_COLS), np.float32)

    def put(name, a):
        lo, hi = CONSTS[name]
        out[:a.shape[0], lo:hi] = a.reshape(a.shape[0], -1)

    put("ident", np.eye(128, dtype=np.float32))
    p, lt, w = np.ogrid[0:128, 0:2, 0:128]
    reach = (128 * lt + p) - ((TOKENS - 128) * lt + w)
    put("band", ((reach >= 0) & (reach < WIN)).astype(np.float32))
    row, b, lt, p = np.ogrid[0:32, 0:2, 0:2, 0:128]
    put("spread", (row == b * WIN + (128 * lt + p) % WIN).astype(np.float32))
    tmap = np.eye(C, dtype=np.float32)
    tmap[C - 1, :] = -1.0
    tmap[:, C - 1] = 0.0
    put("tmap", tmap)
    e, f = np.ogrid[0:EXPERTS, 0:EXPERTS]
    put("lower", np.broadcast_to((f < e).astype(np.float32), (128, EXPERTS, EXPERTS)))
    put("rankmax", np.broadcast_to(np.arange(EXPERTS, dtype=np.float32) - (EXPERTS - 1 - 2), (128, EXPERTS)))
    row, r, m = np.ogrid[0:128, 0:WIN, 0:32]
    put("vplace", (m == (row // 64) * WIN + r).astype(np.float32))
    return out


def kernel(x, L0_tok_W_qry, L0_tok_W_key, L0_tok_v, L0_tok_b, L0_attn_WQ, L0_attn_WK, L0_attn_WV, L0_attn_Wout,
           L0_attn_bout, L0_ffn_Wg, L0_ffn_bg, L0_ffn_W1, L0_ffn_b1, L0_ffn_W2, L0_ffn_b2):
    import concourse.bacc as bacc
    from concourse.bass_utils import run_bass_kernel_spmd

    def lay(a, axes=None, shape=None):
        a = np.asarray(a)
        a = a if axes is None else a.transpose(axes)
        return np.ascontiguousarray(a if shape is None else a.reshape(shape))

    col = (-1, 1)
    arrays = {
        "x": lay(x), "W_qry": lay(L0_tok_W_qry), "W_key": lay(L0_tok_W_key), "v": lay(L0_tok_v, None, col),
        "b": lay(L0_tok_b, None, col), "WQ": lay(L0_attn_WQ), "WK": lay(L0_attn_WK), "WV": lay(L0_attn_WV),
        "Wout": lay(L0_attn_Wout), "bout": lay(L0_attn_bout, None, col),
        "WgT": lay(L0_ffn_Wg, (1, 0)), "bg": lay(L0_ffn_bg, None, col),
        "W1T": lay(L0_ffn_W1, (2, 0, 1), (C, EXPERTS * HID)),
        "b1T": lay(np.asarray(L0_ffn_b1).reshape(2 * EXPERTS, 128), (1, 0)),
        "W2T": lay(np.asarray(L0_ffn_W2).reshape(EXPERTS, C, 2, 128), (3, 0, 2, 1), (128, 2 * EXPERTS, C)),
        "b2T": lay(np.asarray(L0_ffn_b2).reshape(EP, 128), (1, 0)),
        "const": constants(),
    }
    nc = bacc.Bacc("TRN2", target_bir_lowering=False, num_devices=1)
    io = {name: nc.dram_tensor(f"in_{name}", a.shape, F32, kind="ExternalInput").ap() for name, a in arrays.items()}
    io["out"] = nc.dram_tensor("out", (BATCH, TOKENS, C), F32, kind="ExternalOutput").ap()
    audio_tower(nc, io)
    r = run_bass_kernel_spmd(nc, [{f"in_{name}": a for name, a in arrays.items()}], core_ids=[0])
    return r.results[0]["out"]
```

```python
import concourse.bass as bass
import concourse.mybir as mybir
import numpy as np
from contextlib import ExitStack

F32 = mybir.dt.float32
F32R = mybir.dt.float32r
BF16 = mybir.dt.bfloat16
I32 = mybir.dt.int32
ALU = mybir.AluOpType
ACT = mybir.ActivationFunctionType
AX = mybir.AxisListType

BATCH, LENGTH, C = 64, 256, 64
WIN = 9
TOKENS = LENGTH - WIN + 1
HALF = TOKENS // 2
PAIR = 2 * TOKENS
HEADS, HP = 8, 4
EXPERTS, HID = 8, 256
EP = EXPERTS // 2
PAIRS = BATCH // 2
QUARTER = 63
PADDED = 4 * QUARTER
EPS = 1e-5
ATTN_SCALE = float(np.float32(1.0) / np.sqrt(np.float32(8.0)).astype(np.float32))
RSQRT_GUESS = 0x5F3759DF

GLANCE, WINDOW, GRAM, ATTEND, SETTLE, MIX = "glance", "window", "gram", "attend", "settle", "mix"
LAG = {GLANCE: 0, WINDOW: 1, GRAM: 1, ATTEND: 2, SETTLE: 3, MIX: 4}
TURNS = PAIRS + LAG[MIX]
STEADY = LAG[MIX]
LOOP_FROM, LOOP_TO = STEADY + 2, PAIRS

BIG_ORDER = [("l1_0", MIX), ("l1_1", MIX), ("un0", SETTLE), ("un1", SETTLE), ("l1_2", MIX), ("l1_3", MIX),
             ("ub0", SETTLE), ("ub1", SETTLE), ("l1_4", MIX), ("s0", ATTEND), ("l1_5", MIX), ("s1", ATTEND),
             ("l1_6", MIX), ("s2", ATTEND), ("l1_7", MIX), ("s3", ATTEND), ("g0", GRAM), ("g1", GRAM),
             ("s4", ATTEND), ("yn0", MIX), ("yn1", MIX), ("g2", GRAM), ("g3", GRAM), ("s5", ATTEND),
             ("mx0", GRAM), ("mx1", GRAM), ("mx2", GRAM), ("mx3", GRAM), ("s6", ATTEND), ("mx4", GRAM),
             ("s7", ATTEND), ("mx5", GRAM), ("mx6", GRAM), ("mx7", GRAM)]
SUM_ORDER = [("l2_0", MIX), ("l2_1", MIX), ("l2_2", MIX), ("av0", ATTEND), ("l2_3", MIX), ("av1", ATTEND),
             ("av2", ATTEND), ("av3", ATTEND)]
TOK_ORDER = [("sc", WINDOW), ("scn", WINDOW), ("et", WINDOW), ("rp", WINDOW), ("agg", WINDOW), ("hn", WINDOW),
             ("nst", WINDOW), ("xt", GLANCE), ("kq", GLANCE), ("mt", GRAM)]
MID_ORDER = [("op", SETTLE), ("h2n", SETTLE), ("n2st", SETTLE), ("gate", SETTLE), ("gaten", SETTLE)]

CONSTS = {}
_at = 0
for _name, _width in (("ident", 128), ("band", 256), ("spread", 512), ("tmap", 64), ("lower", 64), ("rankmax", 8),
                      ("vplace", WIN * 32)):
    CONSTS[_name] = (_at, _at + _width)
    _at += _width
CONST_COLS = _at
CONST_KEPT = CONSTS["vplace"][0]


class Turn:

    def __init__(self, c, j=None):
        self.c, self.j = c, j

    def ago(self, n):
        return Turn(self.c - n, self.j)

    def value(self, per, plus):
        if self.j is None:
            return per * self.c + plus
        return self.j * (2 * per) + (per * self.c + plus)

    def pair(self, stage):
        return Turn(self.c - LAG[stage], self.j)

    def active(self, stage):
        return self.j is not None or 0 <= self.c - LAG[stage] < PAIRS

    @property
    def buf(self):
        return self.c % 2

    def rounds(self, per, plus):
        if self.j is None:
            return per * (self.c // 2) + plus
        return self.j * per + (per * (self.c // 2) + plus)


class Ring:

    def __init__(self, nc, ctx, name, order, slots, banks):
        self.order, self.slots, self.banks = order, slots, banks
        self.filled = [ctx.enter_context(nc.semaphore(f"{name}_filled{n}")) for n in range(slots)]
        self.drained = [ctx.enter_context(nc.semaphore(f"{name}_drained{n}")) for n in range(slots)]

    def use(self, step, turn):
        names = [s for s, _ in self.order]
        if turn.j is None:
            n = sum(Turn(c).active(stage) for c in range(turn.c) for _, stage in self.order)
            n += sum(turn.active(stage) for _, stage in self.order[:names.index(step)])
            return n % self.slots, n // self.slots
        start = sum(Turn(c).active(stage) for c in range(STEADY) for _, stage in self.order)
        n = start + len(names) * (turn.c - STEADY) + names.index(step)
        return n % self.slots, turn.j * (2 * len(names) // self.slots) + n // self.slots


def hold(eng, sem, value):
    if not isinstance(value, int) or value > 0:
        eng.wait_ge(sem, value)


def hi_half(ap):
    return ap.bitcast(BF16).rearrange("p (n two) -> p n two", two=2)[:, :, 1]


def audio_tower(nc, io):
    ctx = ExitStack()
    with ctx:
        def sb(name, shape, dt=F32):
            return ctx.enter_context(nc.sbuf_tensor(name, shape, dt))

        def sem(name):
            return ctx.enter_context(nc.semaphore(name))

        const = sb("const", [128, CONST_KEPT])
        key_w = sb("key_w", [128, 128])
        qry_w = sb("qry_w", [128, 128])
        tok_v = sb("tok_v", [128, 1])
        tok_b = sb("tok_b", [128, 1])
        vplace = sb("vplace", [128, WIN, 32])
        a_hi = sb("a_hi", [128, HEADS, 2, C], F32R)
        a_lo = sb("a_lo", [128, HEADS, 2, C], F32R)
        o_w = sb("o_w", [128, HP, C])
        o_bias = sb("o_bias", [128, 1])
        g_whi = sb("g_whi", [128, 128], F32R)
        g_wlo = sb("g_wlo", [128, 128], F32R)
        g_b = sb("g_b", [128, 1])
        w1_hi = sb("w1_hi", [128, EXPERTS * HID], F32R)
        w1_lo = sb("w1_lo", [128, EXPERTS * HID], F32R)
        b1 = sb("b1", [128, 2 * EXPERTS])
        w2 = sb("w2", [128, 2 * EXPERTS, C])
        b2 = sb("b2", [128, EP])

        xin = sb("xin", [128, 2, 2, 2, C])
        xt = sb("xt", [128, 264])
        kq = sb("kq", [128, 2, 264])
        tanh = sb("tanh", [128, WIN, PADDED])
        sc = sb("sc", [128, 128])
        smax = sb("smax", [QUARTER, 8])
        sexp = sb("sexp", [QUARTER, 8, WIN])
        ssum = sb("ssum", [QUARTER, 8])
        srec = sb("srec", [QUARTER, 8])
        sn = sb("sn", [128, 4, 32])
        wt = sb("wt", [32, PADDED])
        band = sb("band", [128, 2, 2, 128])
        ht = sb("ht", [128, 2, TOKENS])
        stat = sb("stat", [HALF, 2, 8, 4])
        cen = sb("cen", [HALF, 4, C])
        sqr = sb("sqr", [HALF, 4, C])
        nn = sb("nn", [HALF, 2, 4, C])
        nhl = sb("nhl", [HALF, 4, 2 * C], F32R)
        nst = sb("nst", [128, 2, PAIR], F32R)
        g_hi = sb("g_hi", [128, 2, HEADS, PAIR], F32R)
        g_lo = sb("g_lo", [128, 2, HEADS, PAIR], F32R)
        mx = sb("mx", [128, 2, HEADS, 2])
        mneg = sb("mneg", [16, TOKENS], F32R)
        prob = sb("prob", [128, 4, 4 * TOKENS])
        ut = sb("ut", [128, 2, HP, TOKENS])
        rden = sb("rden", [HALF, 2, 2 * HEADS])
        room = sb("room", [HALF, 4, 8, C])
        un = room[:, :, :, :].rearrange("p (b k) h c -> p b k (h c)", b=2)
        yw = room
        utn = sb("utn", [128, HP, PAIR])
        h2t = sb("h2t", [128, TOKENS])
        h2 = sb("h2", [HALF, 2, 4, C])
        n2 = sqr
        n2hl = sb("n2hl", [HALF, 4, 2 * C], F32R)
        n2st = sb("n2st", [128, 2, PAIR], F32R)
        gt = sb("gt", [128, PAIR])
        lg = sb("lg", [HALF, 4, EXPERTS])
        gmax = sb("gmax", [HALF, 4])
        gexp = sb("gexp", [HALF, 4, EXPERTS])
        beats = sb("beats", [HALF, 4, EXPERTS, EXPERTS])
        duel = sb("duel", [HALF, 4, EXPERTS, EXPERTS])
        rank = sb("rank", [HALF, 4, EXPERTS])
        comb = sb("comb", [HALF, 2, 4, EXPERTS])
        hid = sb("hid", [128, 4, 2, PAIR])
        yt = sb("yt", [128, EP, PAIR])
        res = sb("res", [HALF, 2, 4, C])

        psum = ctx.enter_context(nc.psum_tensor("psum", [128, 8, 512], F32))
        big = Ring(nc, ctx, "big", BIG_ORDER, 2, 2)
        sums = Ring(nc, ctx, "sums", SUM_ORDER, 2, 1)
        tok = Ring(nc, ctx, "tok", TOK_ORDER, 1, 1)
        mid = Ring(nc, ctx, "mid", MID_ORDER, 1, 1)

        def big_ps(slot):
            return psum[:, 2 * slot:2 * slot + 2, :]

        def sum_ps(slot):
            return psum[:, 4 + slot, :]

        tok_ps, mid_ps = psum[:, 6, :], psum[:, 7, :]

        def cst(name, rows=128):
            a, b = CONSTS[name]
            return const[0:rows, a:b]

        ident = cst("ident")
        wq_in = prob[0:64, 0, 0:512]
        wk_in = prob[0:64, 1, 0:512]
        wv_in = prob[0:64, 2, 0:512]
        wo_in = prob[:, 3, 0:HP * C].rearrange("p (h c) -> p h c", h=HP)
        a_all = ut[:, 0, :, :].rearrange("p h s -> p (h s)")[:, 0:HEADS * C]
        utn_flat = utn[:, :, :].rearrange("p e n -> p (e n)")
        wq_map = utn_flat[:, 0:2 * HP * C].rearrange("p (h k c) -> p h k c", h=HP, k=2)
        wkv_map = utn_flat[:, 2 * HP * C:4 * HP * C].rearrange("p (k h c) -> p k h c", k=2, h=HP)
        g_w = hid[:, 3, 0, 0:128]
        w1_in = hid[:, 0:3, :, :].rearrange("p a b n -> p (a b n)")[:, 0:EXPERTS * HID]

        zeroed = sem("zeroed")
        loaded = sem("loaded")
        w_mapped_pe = sem("w_mapped_pe")
        w_mapped = sem("w_mapped")
        x_loaded = [sem("x_loaded0"), sem("x_loaded1")]
        t_summed = sem("t_summed")
        tanh_done = sem("tanh_done")
        s_shifted = sem("s_shifted")
        s_exped = sem("s_exped")
        s_normed = sem("s_normed")
        n_split = sem("n_split")
        g_hi_done = sem("g_hi_done")
        m_stored = [sem("m_stored0"), sem("m_stored1")]
        h2_ready = sem("h2_ready")
        n2_split = sem("n2_split")
        gate_shifted = sem("gate_shifted")
        gate_exped = sem("gate_exped")
        comb_ready = sem("comb_ready")
        y_summed = sem("y_summed")
        out_ready = sem("out_ready")
        out_stored = [sem("out_stored0"), sem("out_stored1")]
        dve_step = sem("dve_step")

        x_v = io["x"].rearrange("(j u b) (lt p) c -> j u p lt b c", u=2, b=2, p=128)
        out_v = io["out"].rearrange("(j u b) (half r) c -> j u r half b c", u=2, b=2, r=HALF)

        block = ctx.enter_context(nc.Block())
        N_LOADS = 24

        def turns(eng, run):
            for c in range(LOOP_FROM):
                run(Turn(c))
            with eng.Fori(LOOP_FROM // 2, LOOP_TO // 2) as j:
                run(Turn(0, j))
                run(Turn(1, j))
            for c in range(LOOP_TO, TURNS):
                run(Turn(c))

        @block.sync
        def _(sp):
            loads = [(const[:, :], io["const"][:, 0:CONST_KEPT]),
                     (vplace[:, :, :], io["const"][:, CONST_KEPT:].rearrange("p (r m) -> p r m", m=32)),
                     (tok_v[0:64, :], io["v"]), (tok_v[64:128, :], io["v"]),
                     (tok_b[0:64, :], io["b"]), (tok_b[64:128, :], io["b"]),
                     (wq_in, io["WQ"]), (wk_in, io["WK"]), (wv_in, io["WV"]),
                     (wo_in, io["Wout"].rearrange("(h p) c -> p h c", p=128)),
                     (o_bias[0:64, :], io["bout"]), (o_bias[64:128, :], io["bout"]),
                     (w1_in[0:64, :], io["W1T"]), (w1_in[64:128, :], io["W1T"]), (b1[:, :], io["b1T"]),
                     (w2[:, :, :], io["W2T"]), (b2[:, :], io["b2T"])]
            for to, of in loads:
                sp.dma_start(to, of).then_inc(loaded, 16)
            sp.wait_ge(zeroed, 1)
            for w, name in ((key_w, "W_key"), (qry_w, "W_qry")):
                for b in range(2):
                    sp.dma_start(w[64 * b:64 * b + 64, 64 * b:64 * b + 64], io[name]).then_inc(loaded, 16)
            for to, of in ((g_w[0:64, 0:EXPERTS], io["WgT"]), (g_w[64:128, 0:EXPERTS], io["WgT"]),
                           (g_b[0:EXPERTS, :], io["bg"])):
                sp.dma_start(to, of).then_inc(loaded, 16)
            assert len(loads) + 4 + 3 == N_LOADS

            def dram(view, turn):
                if turn.j is None:
                    return view[turn.c // 2:turn.c // 2 + 1, turn.buf]
                return view[bass.ds(turn.j + turn.c // 2, 1), turn.buf]

            def run(turn):
                if turn.active(GLANCE):
                    p = turn.pair(GLANCE)
                    if turn.j is not None or p.c >= 2:
                        sp.wait_ge(tok.filled[0], tok.use("agg", turn.ago(1))[1] + 1)
                    for b in range(2):
                        sp.dma_start(xin[:, p.buf, :, b, :],
                                     dram(x_v, p)[:, :, :, b, :].rearrange("a p l c -> p (a l) c")
                                     ).then_inc(x_loaded[p.buf], 16)
                if turn.active(MIX):
                    p = turn.pair(MIX)
                    sp.wait_ge(out_ready, p.value(1, 1))
                    for b in range(2):
                        sp.dma_start(dram(out_v, p)[:, :, :, b, :].rearrange("a r h c -> r (a h) c"),
                                     res[:, p.buf, :, :].rearrange("r (h b) c -> r h b c", b=2)[:, :, b, :]
                                     ).then_inc(out_stored[p.buf], 16)
                if turn.active(GRAM):
                    p = turn.pair(GRAM)
                    slot, n = tok.use("mt", turn)
                    sp.wait_ge(tok.drained[slot], n + 1)
                    sp.dma_start(g_hi[63:64, p.buf, :, :].bitcast(F32).rearrange("o h (b s) -> o (h b) s", b=2),
                                 mneg[:, :].bitcast(F32)).then_inc(m_stored[p.buf], 16)

            turns(sp, run)
            for n in range(2):
                sp.wait_ge(out_stored[n], 32 * (PAIRS // 2))

        @block.gpsimd
        def _(pool):
            def run(turn):
                if turn.active(MIX):
                    p = turn.pair(MIX)
                    for half in range(2):
                        slot, n = big.use(f"yn{half}", turn)
                        pool.wait_ge(big.drained[slot], n + 1)
                        q = yw[:, 2 * half:2 * half + 2]
                        step = p.value(8, 4 * half)
                        for i, width in enumerate((4, 2, 1)):
                            nc.gpsimd.tensor_tensor(q[:, :, 0:width, :], q[:, :, 0:width, :],
                                                    q[:, :, width:2 * width, :], ALU.add).then_inc(y_summed, 1)
                            pool.wait_ge(y_summed, step + i + 1)
                        if half == 0:
                            hold(pool, out_stored[p.buf], p.rounds(32, 0))
                        last = nc.gpsimd.tensor_tensor(res[:, p.buf, 2 * half:2 * half + 2, :], q[:, :, 0, :],
                                                       h2[:, p.buf, 2 * half:2 * half + 2, :], ALU.add)
                        if half == 0:
                            last.then_inc(y_summed, 1)
                        else:
                            last.then_inc(out_ready, 1)
                            pool.wait_ge(out_ready, p.value(1, 1))
                            pool.sem_inc(y_summed, 1)
                if turn.active(GLANCE):
                    p = turn.pair(GLANCE)
                    slot, n = tok.use("kq", turn)
                    pool.wait_ge(tok.drained[slot], n + 1)
                    if turn.active(WINDOW):
                        pool.wait_ge(tok.filled[0], tok.use("sc", turn)[1] + 1)
                    rows = PADDED // WIN
                    q = kq[:, 1, 0:PADDED].rearrange("p (a e) -> p a e", e=WIN)
                    k = kq[:, 0, 0:PADDED + WIN].rearrange("p (a e) -> p a e", e=WIN)
                    for r in range(WIN):
                        t = tanh[:, r, :].rearrange("p (a e) -> p a e", e=WIN)
                        last = nc.gpsimd.tensor_tensor(t[:, :, 0:r + 1], q[:, :, 0:r + 1],
                                                       k[:, 0:rows, r:r + 1].broadcast_to([128, rows, r + 1]),
                                                       ALU.add)
                        if r < WIN - 1:
                            nc.gpsimd.tensor_tensor(t[:, :, r + 1:WIN], q[:, :, r + 1:WIN],
                                                    k[:, 1:rows + 1, r:r + 1].broadcast_to([128, rows, WIN - 1 - r]),
                                                    ALU.add)
                    last.then_inc(t_summed, 1)

            turns(pool, run)

        @block.scalar
        def _(act):
            act.wait_ge(loaded, 16 * N_LOADS)

            def relu(turn, e):
                slot, n = big.use(f"l1_{e}", turn)
                if e >= 4:
                    if e % 2 == 0:
                        s, m = sums.use(f"l2_{(e - 4) // 2}", turn)
                        act.wait_ge(sums.filled[s], m + 1)
                elif e % 2 == 0 and turn.pair(MIX).active(GLANCE) and (turn.j is not None or turn.pair(MIX).c >= 1):
                    s, m = sums.use(f"l2_{2 + e // 2}", turn.ago(1))
                    act.wait_ge(sums.filled[s], m + 1)
                act.wait_ge(big.filled[slot], n + 1)
                for c in range(2):
                    last = nc.scalar.activation(hid[:, e % 4, c, :], big_ps(slot)[:, c, 0:PAIR], ACT.Relu,
                                                bias=b1[:, 2 * e + c:2 * e + c + 1])
                last.then_inc(big.drained[slot], 1)

            def expert_out(turn, ep):
                slot, n = sums.use(f"l2_{ep}", turn)
                if ep == 0 and (turn.j is not None or turn.pair(MIX).c >= 1):
                    s, m = big.use("yn1", turn.ago(1))
                    act.wait_ge(big.filled[s], m + 1)
                act.wait_ge(sums.filled[slot], n + 1)
                nc.scalar.activation(yt[:, ep, :], sum_ps(slot)[:, 0:PAIR], ACT.Identity,
                                     bias=b2[:, ep:ep + 1]).then_inc(sums.drained[slot], 1)

            def attn_back(turn, g):
                slot, n = big.use(f"ub{g}", turn)
                if g == 0 and (turn.j is not None or turn.pair(SETTLE).c >= 1):
                    act.wait_ge(mid.filled[0], mid.use("op", turn.ago(1))[1] + 1)
                act.wait_ge(big.filled[slot], n + 1)
                nc.scalar.activation(utn[:, 2 * g:2 * g + 2, :], big_ps(slot)[:, :, 0:PAIR], ACT.Copy
                                     ).then_inc(big.drained[slot], 1)

            def scores_exp(turn, i):
                p = turn.pair(ATTEND)
                slot, n = big.use(f"s{i}", turn)
                if i % 2 == 0 and (i >= 4 or turn.j is not None or p.c >= 1):
                    s, m = sums.use(f"av{(i // 2 + 2) % 4}", turn if i >= 4 else turn.ago(1))
                    act.wait_ge(sums.filled[s], m + 1)
                act.wait_ge(big.filled[slot], n + 1)
                nc.scalar.activation(prob[0:HALF, i % 4, :].rearrange("p (k n) -> p k n", k=2),
                                     big_ps(slot)[0:HALF, :, 0:PAIR], ACT.Exp).then_inc(big.drained[slot], 1)

            def attn_sums(turn, i):
                slot, n = sums.use(f"av{i}", turn)
                if i % 2 == 0 and turn.active(SETTLE):
                    s, m = big.use(f"un{i // 2}", turn)
                    act.wait_ge(big.filled[s], m + 1)
                act.wait_ge(sums.filled[slot], n + 1)
                nc.scalar.activation(ut[:, i // 2, 2 * (i % 2):2 * (i % 2) + 2, :],
                                     sum_ps(slot)[:, 0:PAIR].rearrange("p (k n) -> p k n", k=2), ACT.Copy
                                     ).then_inc(sums.drained[slot], 1)

            def window_exp(turn):
                act.wait_ge(s_shifted, turn.pair(WINDOW).value(1, 1))
                nc.scalar.activation(sexp[:, :, :], sexp[:, :, :], ACT.Exp).then_inc(s_exped, 1)

            def residual(turn):
                p = turn.pair(SETTLE)
                slot, n = mid.use("h2n", turn)
                hold(act, out_ready, p.value(1, -1))
                act.wait_ge(mid.filled[slot], n + 1)
                nc.scalar.activation(h2[:, p.buf, :, :].rearrange("p q c -> p (q c)"),
                                     mid_ps[0:HALF, 0:4 * C], ACT.Copy).then_inc(mid.drained[slot], 1)

            def norm1_cols(turn):
                p = turn.pair(WINDOW)
                if turn.j is not None or p.c >= 2:
                    s, m = big.use("s7", turn.ago(1))
                    act.wait_ge(big.filled[s], m + 1)
                slot, n = tok.use("nst", turn)
                act.wait_ge(tok.filled[slot], n + 1)
                nc.scalar.activation(nst[:, p.buf, :], tok_ps[:, 0:PAIR], ACT.Copy).then_inc(tok.drained[slot], 1)

            def norm2_cols(turn):
                p = turn.pair(SETTLE)
                slot, n = mid.use("n2st", turn)
                if turn.j is not None or p.c >= 2:
                    s, m = big.use("l1_7", turn.ago(1))
                    act.wait_ge(big.filled[s], m + 1)
                act.wait_ge(mid.filled[slot], n + 1)
                nc.scalar.activation(n2st[:, p.buf, :], mid_ps[:, 0:PAIR], ACT.Copy).then_inc(mid.drained[slot], 1)

            def gate_bias(turn):
                slot, n = mid.use("gate", turn)
                act.wait_ge(mid.filled[slot], n + 1)
                nc.scalar.activation(gt[:, :], mid_ps[:, 0:PAIR], ACT.Identity, bias=g_b[:, :]
                                     ).then_inc(mid.drained[slot], 1)

            def gate_exp(turn):
                act.wait_ge(gate_shifted, turn.pair(SETTLE).value(1, 1))
                nc.scalar.activation(gexp[:, :, :], gexp[:, :, :], ACT.Exp).then_inc(gate_exped, 1)

            def gram_hi(turn, g):
                p = turn.pair(GRAM)
                slot, n = big.use(f"g{g}", turn)
                if g == 0 and (turn.j is not None or p.c >= 2):
                    s, m = big.use("s7", turn.ago(1))
                    act.wait_ge(big.filled[s], m + 1)
                act.wait_ge(big.filled[slot], n + 1)
                nc.scalar.activation(g_hi[:, p.buf, 2 * g:2 * g + 2, :], big_ps(slot)[:, :, 0:PAIR], ACT.Copy
                                     ).then_inc(g_hi_done, 1)

            def window_tanh(turn):
                act.wait_ge(t_summed, turn.pair(GLANCE).value(1, 1))
                t = tanh[:, :, :].rearrange("p r w -> p (r w)")
                nc.scalar.activation(t, t, ACT.Tanh, bias=tok_b[:, :]).then_inc(tanh_done, 1)

            def maxima(turn):
                p = turn.pair(GRAM)
                slot, n = tok.use("mt", turn)
                if turn.j is not None or p.c >= 1:
                    act.wait_ge(m_stored[(p.c + 1) % 2], p.ago(1).rounds(16, 16))
                act.wait_ge(tok.filled[slot], n + 1)
                nc.scalar.activation(mneg[:, :], tok_ps[0:16, 0:TOKENS], ACT.Copy, scale=-1.0
                                     ).then_inc(tok.drained[slot], 1)

            def run(turn):
                win, glance, gram = turn.active(WINDOW), turn.active(GLANCE), turn.active(GRAM)
                attend, settle, mix = turn.active(ATTEND), turn.active(SETTLE), turn.active(MIX)
                mix and relu(turn, 0)
                mix and relu(turn, 1)
                win and window_exp(turn)
                mix and relu(turn, 2)
                mix and relu(turn, 3)
                settle and attn_back(turn, 0)
                settle and attn_back(turn, 1)
                mix and relu(turn, 4)
                attend and scores_exp(turn, 0)
                mix and expert_out(turn, 0)
                mix and relu(turn, 5)
                settle and residual(turn)
                attend and scores_exp(turn, 1)
                mix and expert_out(turn, 1)
                mix and relu(turn, 6)
                attend and scores_exp(turn, 2)
                win and norm1_cols(turn)
                mix and expert_out(turn, 2)
                mix and relu(turn, 7)
                attend and scores_exp(turn, 3)
                gram and gram_hi(turn, 0)
                gram and gram_hi(turn, 1)
                attend and attn_sums(turn, 0)
                mix and expert_out(turn, 3)
                attend and scores_exp(turn, 4)
                gram and gram_hi(turn, 2)
                gram and gram_hi(turn, 3)
                attend and scores_exp(turn, 5)
                attend and attn_sums(turn, 1)
                settle and norm2_cols(turn)
                attend and scores_exp(turn, 6)
                settle and gate_bias(turn)
                attend and scores_exp(turn, 7)
                glance and window_tanh(turn)
                attend and attn_sums(turn, 2)
                settle and gate_exp(turn)
                gram and maxima(turn)
                attend and attn_sums(turn, 3)

            turns(act, run)

        @block.vector
        def _(dve):
            count = {"base": 0, "n": 0}

            def link(ins):
                count["n"] += 1
                ins.then_inc(dve_step, 1)
                dve.wait_ge(dve_step, count["base"] + count["n"])

            V = nc.vector
            for t in (key_w[:, :], qry_w[:, :], xt[:, :], kq[:, :, :], sc[:, :], sn[:, :, :], g_w, g_b[:, :]):
                V.memset(t, 0.0)
            V.memset(nn[:, :, :, C - 1:C], 1.0).then_inc(zeroed, 1)
            dve.wait_ge(loaded, 16 * N_LOADS)
            V.tensor_scalar(vplace[:, :, :], vplace[:, :, :], tok_v[:, 0:1], None,
                            ALU.mult)
            for hi, lo, of in ((w1_hi, w1_lo, w1_in), (g_whi, g_wlo, g_w)):
                link(V.tensor_copy(hi[:, :], of))
                link(V.tensor_tensor(lo[:, :], of, hi[:, :], ALU.subtract))
            dve.wait_ge(w_mapped_pe, 1)
            V.tensor_copy(wq_map[:, :, :, :], psum[:, 0, 0:HP * C].rearrange("p (h o c) -> p h o c", h=HP, o=1)
                          .broadcast_to([128, HP, 2, C]))
            V.tensor_copy(wkv_map[:, :, :, :].rearrange("p k h c -> p (k h c)"), psum[:, 1, 0:2 * HP * C]
                          ).then_inc(w_mapped, 1)
            dve.wait_ge(w_mapped_pe, 2)
            for par in range(2):
                V.tensor_scalar(a_all.rearrange("p (h k c) -> p h k c", h=HP, k=2)[:, :, par, :],
                                psum[:, 2 + par, 0:HP * C].rearrange("p (h c) -> p h c", h=HP),
                                ATTN_SCALE, None, ALU.mult)
                last = V.tensor_copy(o_w[64 * par:64 * par + 64, :, :].rearrange("p h c -> p (h c)"),
                                     psum[64 * par:64 * par + 64, 4 + par, 0:HP * C])
            link(last)
            a_twice = a_all.rearrange("p (h o c) -> p h o c", o=1, c=C).broadcast_to([128, HEADS, 2, C])
            link(V.tensor_copy(a_hi[:, :, :, :], a_twice))
            V.tensor_tensor(a_lo[:, :, :, :], a_twice, a_hi[:, :, :, :], ALU.subtract).then_inc(w_mapped, 1)

            def layer_norm(which, src, to, width, freed=None):
                s = stat[:, which]
                c, q = cen[:, :, :], sqr[:, :, :]
                link(V.tensor_reduce(s[:, 0, :], src, AX.X, ALU.add))
                link(V.tensor_scalar(s[:, 1, :], s[:, 0, :], -1.0 / C, None, ALU.mult))
                ins = V.tensor_tensor(c, src, s[:, 1, :].rearrange("p (q o) -> p q o", o=1)
                                      .broadcast_to([HALF, 4, C]), ALU.add)
                if freed is None:
                    link(ins)
                else:
                    ins.then_inc(freed[0], 1)
                    dve.wait_ge(freed[0], freed[1])
                link(V.tensor_tensor(q, c, c, ALU.mult))
                link(V.tensor_reduce(s[:, 2, :], q, AX.X, ALU.add))
                link(V.tensor_scalar(s[:, 2, :], s[:, 2, :], 1.0 / C, EPS, ALU.mult, ALU.add))
                v, y, t = s[:, 2, :], s[:, 3, :], s[:, 4, :]
                link(V.tensor_single_scalar(y.bitcast(I32), v.bitcast(I32), 1, ALU.logical_shift_right))
                link(V.tensor_scalar(y.bitcast(I32), y.bitcast(I32), -1.0, float(RSQRT_GUESS), ALU.mult, ALU.add))
                for _ in range(3):
                    link(V.scalar_tensor_tensor(t, y, -0.5, y, ALU.mult, ALU.mult))
                    link(V.tensor_tensor(t, t, v, ALU.mult))
                    link(V.scalar_tensor_tensor(y, t, 1.5, y, ALU.add, ALU.mult))
                link(V.tensor_tensor(to[:, :, 0:width], c[:, :, 0:width],
                                     y.rearrange("p (q o) -> p q o", o=1).broadcast_to([HALF, 4, width]), ALU.mult))

            def normalise(turn, b):
                slot, n = big.use(f"un{b}", turn)
                dve.wait_ge(big.filled[slot], n + 1)
                u = big_ps(slot)[0:HALF].rearrange("p k (h c) -> p (k h) c", c=C)
                link(V.reciprocal(rden[:, b, :], u[:, :, C - 1]))
                if b == 0:
                    hold(dve, out_ready, turn.pair(MIX).value(1, 0))
                V.tensor_tensor(un[:, b, :, :].rearrange("p k (h c) -> p (k h) c", c=C), u,
                                rden[:, b, :].rearrange("p (h o) -> p h o", o=1).broadcast_to([HALF, 16, C]), ALU.mult
                                ).then_inc(big.drained[slot], 1)

            def weigh(turn, half):
                p = turn.pair(MIX)
                slot, n = big.use(f"yn{half}", turn)
                if half == 0 and turn.active(SETTLE):
                    s, m = big.use("ub1", turn)
                    dve.wait_ge(big.filled[s], m + 1)
                elif half == 0:
                    hold(dve, out_ready, p.value(1, 0))
                dve.wait_ge(comb_ready, p.value(1, 1))
                dve.wait_ge(big.filled[slot], n + 1)
                V.tensor_tensor(yw[:, 2 * half:2 * half + 2].rearrange("p q e c -> p (q e) c"),
                                big_ps(slot)[0:HALF].rearrange("p k (e c) -> p (k e) c", c=C),
                                comb[:, p.buf, 2 * half:2 * half + 2, :].rearrange("p q (e o) -> p (q e) o", o=1)
                                .broadcast_to([HALF, 16, C]), ALU.mult).then_inc(big.drained[slot], 1)

            def row_max(turn, i):
                four, b, st = i // 4, i // 2 % 2, i % 2
                slot, n = big.use(f"mx{i}", turn)
                if i == 0 and (turn.j is not None or turn.pair(GRAM).c >= 1):
                    dve.wait_ge(tok.filled[0], tok.use("mt", turn.ago(1))[1] + 1)
                dve.wait_ge(big.filled[slot], n + 1)
                V.tensor_reduce(mx[:, st, 4 * four:4 * four + 4, b].rearrange("p (k h) -> p k h", k=2),
                                big_ps(slot)[:, :, 0:PAIR].rearrange("p k (h s) -> p k h s", h=2),
                                AX.X, ALU.max).then_inc(big.drained[slot], 1)

            def tok_copy(turn, step, to, of):
                slot, n = tok.use(step, turn)
                dve.wait_ge(tok.filled[slot], n + 1)
                V.tensor_copy(to, of).then_inc(tok.drained[slot], 1)

            def softmax_shift(turn):
                slot, n = tok.use("scn", turn)
                dve.wait_ge(tok.filled[slot], n + 1)
                s = (tok_ps[0:QUARTER, 0:128].rearrange("p (j m) -> p j m", m=32)[:, :, 0:2 * WIN]
                     .rearrange("p j (b r) -> p j b r", b=2))
                link(V.tensor_reduce(smax[:, :].rearrange("p (j b) -> p j b", b=2), s, AX.X, ALU.max))
                V.tensor_tensor(sexp[:, :, :].rearrange("p (j b) r -> p j b r", b=2), s,
                                smax[:, :].rearrange("p (j b o) -> p j b o", b=2, o=1)
                                .broadcast_to([QUARTER, 4, 2, WIN]), ALU.subtract).then_inc(tok.drained[slot], 1)
                dve.wait_ge(tok.drained[slot], n + 1)
                dve.sem_inc(s_shifted, 1)

            def softmax_norm(turn):
                dve.wait_ge(s_exped, turn.pair(WINDOW).value(1, 1))
                link(V.tensor_reduce(ssum[:, :], sexp[:, :, :], AX.X, ALU.add))
                link(V.reciprocal(srec[:, :], ssum[:, :]))
                V.tensor_tensor(sn[0:QUARTER, :, 0:2 * WIN].rearrange("p j (b r) -> p j b r", b=2),
                                sexp[:, :, :].rearrange("p (j b) r -> p j b r", b=2),
                                srec[:, :].rearrange("p (j b o) -> p j b o", b=2, o=1)
                                .broadcast_to([QUARTER, 4, 2, WIN]), ALU.mult).then_inc(s_normed, 1)

            def band_weights(turn):
                slot, n = tok.use("rp", turn)
                dve.wait_ge(tok.filled[slot], n + 1)
                V.tensor_tensor(band[:, :, :, :].rearrange("p b t w -> p b (t w)"),
                                tok_ps[:, 0:512].rearrange("p (b w) -> p b w", b=2),
                                cst("band").rearrange("p (o w) -> p o w", o=1).broadcast_to([128, 2, 256]),
                                ALU.mult).then_inc(tok.drained[slot], 1)

            def residual(turn):
                slot, n = mid.use("op", turn)
                dve.wait_ge(mid.filled[slot], n + 1)
                V.scalar_tensor_tensor(h2t[:, :], mid_ps[:, 0:TOKENS], o_bias[:, 0:1],
                                       ht[:, turn.pair(SETTLE).buf, :], ALU.add, ALU.add
                                       ).then_inc(mid.drained[slot], 1)

            def window_out(turn):
                if turn.active(SETTLE):
                    slot, n = mid.use("op", turn)
                    dve.wait_ge(mid.drained[slot], n + 1)
                tok_copy(turn, "agg", ht[:, turn.pair(WINDOW).buf, :], tok_ps[:, 0:TOKENS])

            def norm1(turn):
                p = turn.pair(WINDOW)
                slot, n = tok.use("hn", turn)
                dve.wait_ge(tok.filled[slot], n + 1)
                if turn.j is not None or p.c >= 2:
                    s, m = sums.use("av3", turn.ago(1))
                    dve.wait_ge(sums.filled[s], m + 1)
                layer_norm(0, tok_ps[0:HALF, 0:4 * C].rearrange("p (q c) -> p q c", c=C), nn[:, p.buf], C - 1,
                           freed=(tok.drained[slot], n + 1))
                if turn.j is not None or p.c >= 1:
                    dve.wait_ge(tok.filled[0], tok.use("nst", turn.ago(1))[1] + 1)
                link(V.tensor_copy(nhl[:, :, 0:C], nn[:, p.buf]))
                V.tensor_tensor(nhl[:, :, C:2 * C], nn[:, p.buf], nhl[:, :, 0:C], ALU.subtract
                                ).then_inc(n_split, 1)

            def norm2(turn):
                p = turn.pair(SETTLE)
                slot, n = mid.use("h2n", turn)
                dve.wait_ge(mid.drained[slot], n + 1)
                layer_norm(1, h2[:, p.buf], n2, C)
                if turn.j is not None or p.c >= 1:
                    dve.wait_ge(mid.filled[0], mid.use("n2st", turn.ago(1))[1] + 1)
                link(V.tensor_copy(n2hl[:, :, 0:C], n2[:, :, :]))
                V.tensor_tensor(n2hl[:, :, C:2 * C], n2[:, :, :], n2hl[:, :, 0:C], ALU.subtract
                                ).then_inc(n2_split, 1)

            def gate(turn):
                p = turn.pair(SETTLE)
                slot, n = mid.use("gaten", turn)
                dve.wait_ge(mid.filled[slot], n + 1)
                V.tensor_copy(lg[:, :, :], mid_ps[0:HALF, :].rearrange("p (q e) -> p q e", q=4)[:, :, 0:EXPERTS]
                              ).then_inc(mid.drained[slot], 1)
                dve.wait_ge(mid.drained[slot], n + 1)
                link(V.tensor_reduce(gmax[:, :], lg[:, :, :], AX.X, ALU.max))
                V.tensor_tensor(gexp[:, :, :], lg[:, :, :], gmax[:, :].rearrange("p (q o) -> p q o", o=1)
                                .broadcast_to([HALF, 4, EXPERTS]), ALU.subtract).then_inc(gate_shifted, 1)
                every = [HALF, 4, EXPERTS, EXPERTS]
                link(V.tensor_tensor(beats[:, :, :, :],
                                     lg[:, :, :].rearrange("p q (o e) -> p q o e", o=1).broadcast_to(every),
                                     lg[:, :, :].rearrange("p q (e o) -> p q e o", o=1).broadcast_to(every),
                                     ALU.is_ge))
                link(V.tensor_tensor(duel[:, :, :, :].rearrange("p q e f -> p q (e f)"),
                                     beats[:, :, :, :].rearrange("p q e f -> p q (e f)"),
                                     cst("lower", HALF).rearrange("p (o e) -> p o e", o=1)
                                     .broadcast_to([HALF, 4, EXPERTS * EXPERTS]), ALU.mult))
                link(V.tensor_tensor(beats[:, :, :, :], duel[:, :, :, :],
                                     duel[:, :, :, :].rearrange("p q e f -> p q f e"), ALU.subtract))
                link(V.tensor_reduce(rank[:, :, :], beats[:, :, :, :], AX.X, ALU.add))
                link(V.tensor_tensor(rank[:, :, :], rank[:, :, :],
                                     cst("rankmax", HALF).rearrange("p (o e) -> p o e", o=1)
                                     .broadcast_to([HALF, 4, EXPERTS]), ALU.is_lt))
                dve.wait_ge(gate_exped, p.value(1, 1))
                link(V.tensor_tensor(rank[:, :, :], rank[:, :, :], gexp[:, :, :], ALU.mult))
                link(V.tensor_reduce(gmax[:, :], rank[:, :, :], AX.X, ALU.add))
                link(V.reciprocal(gmax[:, :], gmax[:, :]))
                V.tensor_tensor(comb[:, p.buf], rank[:, :, :], gmax[:, :].rearrange("p (q o) -> p q o", o=1)
                                .broadcast_to([HALF, 4, EXPERTS]), ALU.mult).then_inc(comb_ready, 1)

            def gram_lo(turn, g):
                p = turn.pair(GRAM)
                slot, n = big.use(f"g{g}", turn)
                dve.wait_ge(g_hi_done, p.value(4, g + 1))
                V.tensor_tensor(g_lo[:, p.buf, 2 * g:2 * g + 2, :], big_ps(slot)[:, :, 0:PAIR],
                                g_hi[:, p.buf, 2 * g:2 * g + 2, :], ALU.subtract).then_inc(big.drained[slot], 1)

            def keys_queries(turn):
                hold(dve, t_summed, turn.pair(GLANCE).value(1, 0))
                tok_copy(turn, "kq", kq[:, :, 0:LENGTH], tok_ps[:, 0:512].rearrange("p (k n) -> p k n", k=2))

            def run(turn):
                win, glance, gram = turn.active(WINDOW), turn.active(GLANCE), turn.active(GRAM)
                settle, mix = turn.active(SETTLE), turn.active(MIX)
                win and tok_copy(turn, "sc", sc[:, 0:QUARTER], tok_ps[:, 0:QUARTER])
                settle and normalise(turn, 0)
                win and softmax_shift(turn)
                settle and normalise(turn, 1)
                win and softmax_norm(turn)
                win and tok_copy(turn, "et", wt[:, :], tok_ps[0:32, 0:PADDED])
                win and band_weights(turn)
                settle and residual(turn)
                win and window_out(turn)
                win and norm1(turn)
                settle and norm2(turn)
                gram and gram_lo(turn, 0)
                gram and gram_lo(turn, 1)
                mix and weigh(turn, 0)
                mix and weigh(turn, 1)
                gram and gram_lo(turn, 2)
                gram and gram_lo(turn, 3)
                glance and tok_copy(turn, "xt", xt[:, 0:LENGTH], tok_ps[:, 0:LENGTH])
                gram and row_max(turn, 0)
                glance and keys_queries(turn)
                gram and row_max(turn, 1)
                gram and row_max(turn, 2)
                gram and row_max(turn, 3)
                gram and row_max(turn, 4)
                gram and row_max(turn, 5)
                gram and row_max(turn, 6)
                gram and row_max(turn, 7)
                settle and gate(turn)

            def counted(turn):
                count["base"], count["n"] = count["base"] + count["n"], 0
                run(turn)

            for c in range(LOOP_FROM):
                counted(Turn(c))
            start, per = count["base"] + count["n"], count["n"]
            with dve.Fori(LOOP_FROM // 2, LOOP_TO // 2) as j:
                for u in range(2):
                    count["base"], count["n"] = j * (2 * per) + (start - LOOP_FROM * per + u * per), 0
                    run(Turn(u, j))
                    assert count["n"] == per
            count["base"], count["n"] = start + (LOOP_TO - LOOP_FROM) * per, 0
            for c in range(LOOP_TO, TURNS):
                counted(Turn(c))

        @block.tensor
        def _(pe):
            mm = nc.tensor.matmul

            pe.wait_ge(zeroed, 1)
            pe.wait_ge(loaded, 16 * N_LOADS)
            for k, w in enumerate((wq_in, wk_in, wv_in)):
                for hp in range(HP):
                    at = hp * C if k == 0 else ((k - 1) * HP + hp) * C
                    last = mm(psum[:, min(k, 1), at:at + C], w[:, 128 * hp:128 * hp + 128], cst("tmap", 64),
                              start=True, stop=True)
            last.then_inc(w_mapped_pe, 1)
            pe.wait_ge(w_mapped, 1)
            for par in range(2):
                r = slice(64 * par, 64 * par + 64)
                for hp in range(HP):
                    at = slice(hp * C, hp * C + C)
                    mm(psum[:, 2 + par, at], wq_map[r, hp].rearrange("p o c -> p (o c)"), wkv_map[r, 0, hp],
                       start=True, stop=True)
                    last = mm(psum[r, 4 + par, at], wkv_map[r, 1, hp], wo_in[r, hp, :], start=True, stop=True)
            last.then_inc(w_mapped_pe, 1)
            pe.wait_ge(w_mapped, 2)

            def flip(out, of, last=None):
                rows = of.shape[0]
                return nc.tensor.transpose(out, of, ident[0:rows, 0:rows])

            def free(ring, step, turn):
                slot, n = ring.use(step, turn)
                hold(pe, ring.drained[slot], n)
                return slot

            def ln_cols(q):
                at = (q % 2) * TOKENS + (q // 2) * HALF
                return slice(at, at + HALF)

            def attn_rows(turn, b):
                if b == 0:
                    for i in (2, 3):
                        s, m = sums.use(f"av{i}", turn.ago(1))
                        pe.wait_ge(sums.drained[s], m + 1)
                slot = free(big, f"un{b}", turn)
                for half in range(2):
                    for hp in range(HP):
                        last = flip(big_ps(slot)[0:HALF, half, 128 * hp:128 * hp + 128],
                                    ut[:, b, hp, half * HALF:(half + 1) * HALF])
                last.then_inc(big.filled[slot], 1)

            def attn_cols(turn, g):
                if g == 0:
                    for b in range(2):
                        s, m = big.use(f"un{b}", turn)
                        pe.wait_ge(big.drained[s], m + 1)
                slot = free(big, f"ub{g}", turn)
                for k in range(2):
                    for b in range(2):
                        for half in range(2):
                            at = b * TOKENS + half * HALF
                            hp = 2 * g + k
                            last = flip(big_ps(slot)[:, k, at:at + HALF], un[:, b, half, 128 * hp:128 * hp + 128])
                last.then_inc(big.filled[slot], 1)

            def layer1(turn, e):
                p = turn.pair(MIX)
                if e == 0:
                    pe.wait_ge(mid.drained[0], mid.use("n2st", turn.ago(1))[1] + 1)
                slot = free(big, f"l1_{e}", turn)
                for c in range(2):
                    at = slice((2 * e + c) * 128, (2 * e + c + 1) * 128)
                    for w in (w1_hi, w1_lo):
                        last = mm(big_ps(slot)[:, c, 0:PAIR], w[:, at], n2st[:, p.buf, :],
                                  start=(w is w1_hi), stop=(w is w1_lo))
                last.then_inc(big.filled[slot], 1)

            def layer2(turn, ep):
                for e in (2 * ep, 2 * ep + 1):
                    s, m = big.use(f"l1_{e}", turn)
                    pe.wait_ge(big.drained[s], m + 1)
                slot = free(sums, f"l2_{ep}", turn)
                for c in range(2):
                    for par in range(2):
                        e = 2 * ep + par
                        last = mm(sum_ps(slot)[64 * par:64 * par + 64, 0:PAIR], w2[:, 2 * e + c, :],
                                  hid[:, e % 4, c, :], start=(c == 0), stop=(c == 1))
                last.then_inc(sums.filled[slot], 1)

            def yn(turn, half):
                if half == 0:
                    for ep in (2, 3):
                        s, m = sums.use(f"l2_{ep}", turn)
                        pe.wait_ge(sums.drained[s], m + 1)
                slot = free(big, f"yn{half}", turn)
                for b in range(2):
                    for ep in range(EP):
                        last = flip(big_ps(slot)[0:HALF, b, 128 * ep:128 * ep + 128], yt[:, ep, ln_cols(2 * half + b)])
                last.then_inc(big.filled[slot], 1)

            def score(turn, i):
                p = turn.pair(ATTEND)
                b, four, tt = i // 4, i // 2 % 2, i % 2
                keys = slice(b * TOKENS + tt * HALF, b * TOKENS + (tt + 1) * HALF)
                if i == 0:
                    pe.wait_ge(m_stored[p.buf], p.rounds(16, 16))
                slot = free(big, f"s{i}", turn)
                for k in range(2):
                    h = 4 * four + 2 * k
                    for g in (g_hi, g_lo):
                        last = mm(big_ps(slot)[0:HALF, k, 0:PAIR], nst[:, p.buf, keys],
                                  g[:, p.buf, h:h + 2, b * TOKENS:(b + 1) * TOKENS],
                                  start=(g is g_hi), stop=(g is g_lo))
                last.then_inc(big.filled[slot], 1)

            def attend_sum(turn, i):
                p = turn.pair(ATTEND)
                b = i // 2
                for tt in range(2):
                    s, m = big.use(f"s{2 * i + tt}", turn)
                    pe.wait_ge(big.drained[s], m + 1)
                slot = free(sums, f"av{i}", turn)
                for tt in range(2):
                    for par in range(2):
                        last = mm(sum_ps(slot)[64 * par:64 * par + 64, 0:PAIR], nn[:, p.buf, 2 * tt + b, :],
                                  prob[0:HALF, (2 * i + tt) % 4, :].rearrange("p (k r s) -> p k r s", k=2, r=2)[:, :, par, :],
                                  start=(tt == 0), stop=(tt == 1))
                last.then_inc(sums.filled[slot], 1)

            def row_max(turn, i):
                p = turn.pair(GRAM)
                four, b, st = i // 4, i // 2 % 2, i % 2
                slot = free(big, f"mx{i}", turn)
                for h in range(4):
                    at = b * TOKENS + st * (TOKENS - 128)
                    last = mm(big_ps(slot)[:, h // 2, TOKENS * (h % 2):TOKENS * (h % 2) + TOKENS],
                              hi_half(g_hi[:, p.buf, 4 * four + h, at:at + 128]),
                              hi_half(nst[:, p.buf, b * TOKENS:(b + 1) * TOKENS]), start=True, stop=True)
                last.then_inc(big.filled[slot], 1)

            def window_scores(turn):
                pe.wait_ge(tanh_done, turn.pair(WINDOW).value(1, 1))
                free(tok, "sc", turn)
                for r in range(WIN):
                    for qt in range(4):
                        last = mm(tok_ps[32 * qt:32 * qt + 32, 0:QUARTER], vplace[:, r, :],
                                  tanh[:, r, QUARTER * qt:QUARTER * (qt + 1)], start=(r == 0), stop=(r == WIN - 1))
                last.then_inc(tok.filled[0], 1)

            def window_rows(turn):
                free(tok, "scn", turn)
                flip(tok_ps[:, 0:128], sc[:, :]).then_inc(tok.filled[0], 1)

            def window_weights(turn):
                pe.wait_ge(s_normed, turn.pair(WINDOW).value(1, 1))
                free(tok, "et", turn)
                for qt in range(4):
                    last = flip(tok_ps[0:32, QUARTER * qt:QUARTER * qt + 128], sn[:, qt, :])
                last.then_inc(tok.filled[0], 1)

            def window_spread(turn):
                free(tok, "rp", turn)
                spread = cst("spread", 32).rearrange("p (b t l) -> p b t l", b=2, t=2)
                for b in range(2):
                    for lt in range(2):
                        w0 = lt * (TOKENS - 128)
                        last = mm(tok_ps[:, (2 * b + lt) * 128:(2 * b + lt + 1) * 128], spread[:, b, lt, :],
                                  wt[:, w0:w0 + 128], start=True, stop=True)
                last.then_inc(tok.filled[0], 1)

            def window_sum(turn):
                free(tok, "agg", turn)
                for lt in range(2):
                    w0 = lt * (TOKENS - 128)
                    for b in range(2):
                        last = mm(tok_ps[64 * b:64 * b + 64, w0:w0 + 128], xin[:, turn.pair(WINDOW).buf, lt, b, :],
                                  band[:, b, lt, :], start=(lt == 0), stop=(lt == 1), skip_group_check=True)
                last.then_inc(tok.filled[0], 1)

            def h_rows(turn):
                free(tok, "hn", turn)
                for half in range(2):
                    last = flip(tok_ps[0:HALF, 128 * half:128 * half + 128],
                                ht[:, turn.pair(WINDOW).buf, half * HALF:(half + 1) * HALF])
                last.then_inc(tok.filled[0], 1)

            def project(turn):
                for g in range(2):
                    s, m = big.use(f"ub{g}", turn)
                    pe.wait_ge(big.drained[s], m + 1)
                free(mid, "op", turn)
                for hp in range(HP):
                    for b in range(2):
                        last = mm(mid_ps[64 * b:64 * b + 64, 0:TOKENS], o_w[:, hp, :],
                                  utn[:, hp, b * TOKENS:(b + 1) * TOKENS], start=(hp == 0), stop=(hp == HP - 1))
                last.then_inc(mid.filled[0], 1)

            def h2_rows(turn):
                free(mid, "h2n", turn)
                for half in range(2):
                    last = flip(mid_ps[0:HALF, 128 * half:128 * half + 128], h2t[:, half * HALF:(half + 1) * HALF])
                last.then_inc(mid.filled[0], 1)

            def norm1_cols(turn):
                pe.wait_ge(n_split, turn.pair(WINDOW).value(1, 1))
                free(tok, "nst", turn)
                for q in range(4):
                    last = flip(tok_ps[:, ln_cols(q)], nhl[:, q, :].bitcast(F32))
                last.then_inc(tok.filled[0], 1)

            def norm2_cols(turn):
                pe.wait_ge(n2_split, turn.pair(SETTLE).value(1, 1))
                free(mid, "n2st", turn)
                for q in range(4):
                    last = flip(mid_ps[:, ln_cols(q)], n2hl[:, q, :].bitcast(F32))
                last.then_inc(mid.filled[0], 1)

            def gate(turn):
                free(mid, "gate", turn)
                buf = turn.pair(SETTLE).buf
                mm(mid_ps[:, 0:PAIR], g_whi[:, :], n2st[:, buf, :], start=True, stop=False)
                mm(mid_ps[:, 0:PAIR], g_wlo[:, :], n2st[:, buf, :], start=False, stop=True
                   ).then_inc(mid.filled[0], 1)

            def gate_rows(turn):
                free(mid, "gaten", turn)
                for q in range(4):
                    last = flip(mid_ps[0:HALF, 128 * q:128 * (q + 1)], gt[:, ln_cols(q)])
                last.then_inc(mid.filled[0], 1)

            def gram(turn, g):
                if g == 0:
                    pe.wait_ge(tok.drained[0], tok.use("nst", turn)[1] + 1)
                slot = free(big, f"g{g}", turn)
                for k in range(2):
                    for w in (a_hi, a_lo):
                        last = mm(big_ps(slot)[:, k, 0:PAIR], w[:, 2 * g + k, :, :].rearrange("p o c -> p (o c)"),
                                  nst[:, turn.pair(GRAM).buf, :], start=(w is a_hi), stop=(w is a_lo))
                last.then_inc(big.filled[slot], 1)

            def x_cols(turn):
                p = turn.pair(GLANCE)
                pe.wait_ge(x_loaded[p.buf], p.rounds(32, 32))
                free(tok, "xt", turn)
                for lt in range(2):
                    last = flip(tok_ps[:, 128 * lt:128 * lt + 128],
                                xin[:, p.buf, lt, :, :].rearrange("p b c -> p (b c)"))
                last.then_inc(tok.filled[0], 1)

            def keys_queries(turn):
                free(tok, "kq", turn)
                mm(tok_ps[:, 0:LENGTH], key_w[:, :], xt[:, 0:LENGTH], start=True, stop=True)
                mm(tok_ps[:, LENGTH:2 * LENGTH], qry_w[:, :], xt[:, WIN // 2:WIN // 2 + LENGTH],
                   start=True, stop=True).then_inc(tok.filled[0], 1)

            def maxima(turn):
                for i in (6, 7):
                    s, m = big.use(f"mx{i}", turn)
                    pe.wait_ge(big.drained[s], m + 1)
                free(tok, "mt", turn)
                for st in range(2):
                    at = st * (TOKENS - 128)
                    last = flip(tok_ps[0:16, at:at + 128], mx[:, st].rearrange("p h b -> p (h b)"))
                last.then_inc(tok.filled[0], 1)

            def run(turn):
                win, glance, gram_on = turn.active(WINDOW), turn.active(GLANCE), turn.active(GRAM)
                attend, settle, mix = turn.active(ATTEND), turn.active(SETTLE), turn.active(MIX)
                mix and layer1(turn, 0)
                mix and layer1(turn, 1)
                win and window_scores(turn)
                settle and attn_rows(turn, 0)
                settle and attn_rows(turn, 1)
                win and window_rows(turn)
                mix and layer2(turn, 0)
                mix and layer1(turn, 2)
                mix and layer1(turn, 3)
                win and window_weights(turn)
                settle and attn_cols(turn, 0)
                win and window_spread(turn)
                settle and attn_cols(turn, 1)
                mix and layer1(turn, 4)
                win and window_sum(turn)
                settle and project(turn)
                attend and score(turn, 0)
                mix and layer1(turn, 5)
                win and h_rows(turn)
                settle and h2_rows(turn)
                attend and score(turn, 1)
                mix and layer2(turn, 1)
                mix and layer1(turn, 6)
                attend and score(turn, 2)
                mix and layer2(turn, 2)
                win and norm1_cols(turn)
                mix and layer1(turn, 7)
                attend and score(turn, 3)
                attend and attend_sum(turn, 0)
                gram_on and gram(turn, 0)
                gram_on and gram(turn, 1)
                mix and layer2(turn, 3)
                attend and score(turn, 4)
                mix and yn(turn, 0)
                mix and yn(turn, 1)
                settle and norm2_cols(turn)
                gram_on and gram(turn, 2)
                glance and x_cols(turn)
                gram_on and gram(turn, 3)
                attend and attend_sum(turn, 1)
                attend and score(turn, 5)
                gram_on and row_max(turn, 0)
                glance and keys_queries(turn)
                gram_on and row_max(turn, 1)
                gram_on and row_max(turn, 2)
                attend and attend_sum(turn, 2)
                gram_on and row_max(turn, 3)
                attend and score(turn, 6)
                gram_on and row_max(turn, 4)
                settle and gate(turn)
                attend and score(turn, 7)
                gram_on and row_max(turn, 5)
                gram_on and row_max(turn, 6)
                settle and gate_rows(turn)
                gram_on and row_max(turn, 7)
                attend and attend_sum(turn, 3)
                gram_on and maxima(turn)

            turns(pe, run)


def constants():
    out = np.zeros((128, CONST_COLS), np.float32)

    def put(name, a):
        lo, hi = CONSTS[name]
        out[:a.shape[0], lo:hi] = a.reshape(a.shape[0], -1)

    put("ident", np.eye(128, dtype=np.float32))
    p, lt, w = np.ogrid[0:128, 0:2, 0:128]
    reach = (128 * lt + p) - ((TOKENS - 128) * lt + w)
    put("band", ((reach >= 0) & (reach < WIN)).astype(np.float32))
    row, b, lt, p = np.ogrid[0:32, 0:2, 0:2, 0:128]
    put("spread", (row == b * WIN + (128 * lt + p) % WIN).astype(np.float32))
    tmap = np.eye(C, dtype=np.float32)
    tmap[C - 1, :] = -1.0
    tmap[:, C - 1] = 0.0
    put("tmap", tmap)
    e, f = np.ogrid[0:EXPERTS, 0:EXPERTS]
    put("lower", np.broadcast_to((f < e).astype(np.float32), (128, EXPERTS, EXPERTS)))
    put("rankmax", np.broadcast_to(np.arange(EXPERTS, dtype=np.float32) - (EXPERTS - 1 - 2), (128, EXPERTS)))
    row, r, m = np.ogrid[0:128, 0:WIN, 0:32]
    put("vplace", (m == (row // 64) * WIN + r).astype(np.float32))
    return out


def kernel(x, L0_tok_W_qry, L0_tok_W_key, L0_tok_v, L0_tok_b, L0_attn_WQ, L0_attn_WK, L0_attn_WV, L0_attn_Wout,
           L0_attn_bout, L0_ffn_Wg, L0_ffn_bg, L0_ffn_W1, L0_ffn_b1, L0_ffn_W2, L0_ffn_b2):
    import concourse.bacc as bacc
    from concourse.bass_utils import run_bass_kernel_spmd

    def lay(a, axes=None, shape=None):
        a = np.asarray(a)
        a = a if axes is None else a.transpose(axes)
        return np.ascontiguousarray(a if shape is None else a.reshape(shape))

    col = (-1, 1)
    arrays = {
        "x": lay(x), "W_qry": lay(L0_tok_W_qry), "W_key": lay(L0_tok_W_key), "v": lay(L0_tok_v, None, col),
        "b": lay(L0_tok_b, None, col), "WQ": lay(L0_attn_WQ), "WK": lay(L0_attn_WK), "WV": lay(L0_attn_WV),
        "Wout": lay(L0_attn_Wout), "bout": lay(L0_attn_bout, None, col),
        "WgT": lay(L0_ffn_Wg, (1, 0)), "bg": lay(L0_ffn_bg, None, col),
        "W1T": lay(L0_ffn_W1, (2, 0, 1), (C, EXPERTS * HID)),
        "b1T": lay(np.asarray(L0_ffn_b1).reshape(2 * EXPERTS, 128), (1, 0)),
        "W2T": lay(np.asarray(L0_ffn_W2).reshape(EXPERTS, C, 2, 128), (3, 0, 2, 1), (128, 2 * EXPERTS, C)),
        "b2T": lay(np.asarray(L0_ffn_b2).reshape(EP, 128), (1, 0)),
        "const": constants(),
    }
    nc = bacc.Bacc("TRN2", target_bir_lowering=False, num_devices=1)
    io = {name: nc.dram_tensor(f"in_{name}", a.shape, F32, kind="ExternalInput").ap() for name, a in arrays.items()}
    io["out"] = nc.dram_tensor("out", (BATCH, TOKENS, C), F32, kind="ExternalOutput").ap()
    audio_tower(nc, io)
    r = run_bass_kernel_spmd(nc, [{f"in_{name}": a for name, a in arrays.items()}], core_ids=[0])
    return r.results[0]["out"]
```

```python
import concourse.bass as bass
import concourse.mybir as mybir
import numpy as np
from contextlib import ExitStack

F32 = mybir.dt.float32
F32R = mybir.dt.float32r
BF16 = mybir.dt.bfloat16
I32 = mybir.dt.int32
ALU = mybir.AluOpType
ACT = mybir.ActivationFunctionType
AX = mybir.AxisListType

BATCH, LENGTH, C = 64, 256, 64
WIN = 9
TOKENS = LENGTH - WIN + 1
HALF = TOKENS // 2
PAIR = 2 * TOKENS
HEADS, HP = 8, 4
EXPERTS, HID = 8, 256
EP = EXPERTS // 2
PAIRS = BATCH // 2
QUARTER = 63
PADDED = 4 * QUARTER
EPS = 1e-5
ATTN_SCALE = float(np.float32(1.0) / np.sqrt(np.float32(8.0)).astype(np.float32))
RSQRT_GUESS = 0x5F3759DF

GLANCE, WINDOW, GRAM, PEAK, ATTEND = "glance", "window", "gram", "peak", "attend"
SETTLE, MIX = "settle", "mix"
LAG = {GLANCE: 0, WINDOW: 1, GRAM: 1, PEAK: 2, ATTEND: 2, SETTLE: 3, MIX: 4}
TURNS = PAIRS + LAG[MIX]
STEADY = LAG[MIX]
LOOP_FROM, LOOP_TO = STEADY + 2, PAIRS

BIG_ORDER = [("l1_0", MIX), ("l1_1", MIX), ("l1_2", MIX), ("l1_3", MIX), ("l1_4", MIX), ("rb0", SETTLE),
             ("rb1", SETTLE), ("l1_5", MIX), ("s0", ATTEND), ("s1", ATTEND), ("s2", ATTEND), ("s3", ATTEND),
             ("l1_6", MIX), ("s4", ATTEND), ("s5", ATTEND), ("l1_7", MIX), ("g0", GRAM), ("g1", GRAM),
             ("mx0", GRAM), ("s6", ATTEND), ("mx1", GRAM), ("yn0", MIX), ("yn1", MIX), ("s7", ATTEND),
             ("mx2", GRAM), ("mx3", GRAM), ("g2", GRAM), ("g3", GRAM), ("mx4", GRAM), ("mx5", GRAM),
             ("mx6", GRAM), ("mx7", GRAM)]
SUM_ORDER = [("l2_0", MIX), ("l2_1", MIX), ("av0", ATTEND), ("av1", ATTEND), ("l2_2", MIX), ("l2_3", MIX),
             ("av2", ATTEND), ("av3", ATTEND)]
TOK_ORDER = [("sc", WINDOW), ("scn", WINDOW), ("mt", PEAK), ("et", WINDOW), ("rp", WINDOW), ("agg", WINDOW),
             ("hn", WINDOW), ("nst", WINDOW), ("xt", GLANCE), ("kq", GLANCE)]
MID_ORDER = [("op", SETTLE), ("h2n", SETTLE), ("n2st", SETTLE), ("gate", SETTLE), ("gaten", SETTLE)]

CONSTS = {}
_at = 0
for _name, _width in (("ident", 128), ("band", 256), ("spread", 512), ("tmap", 64), ("lower", 64), ("rankmax", 8),
                      ("pick", 16),
                      ("vplace", WIN * 32)):
    CONSTS[_name] = (_at, _at + _width)
    _at += _width
CONST_COLS = _at
CONST_KEPT = CONSTS["vplace"][0]


class Turn:

    def __init__(self, c, j=None):
        self.c, self.j = c, j

    def ago(self, n):
        return Turn(self.c - n, self.j)

    def value(self, per, plus):
        if self.j is None:
            return per * self.c + plus
        return self.j * (2 * per) + (per * self.c + plus)

    def pair(self, stage):
        return Turn(self.c - LAG[stage], self.j)

    def active(self, stage):
        return self.j is not None or 0 <= self.c - LAG[stage] < PAIRS

    @property
    def buf(self):
        return self.c % 2

    def rounds(self, per, plus):
        if self.j is None:
            return per * (self.c // 2) + plus
        return self.j * per + (per * (self.c // 2) + plus)


class Ring:

    def __init__(self, nc, ctx, name, order, slots, banks):
        self.order, self.slots, self.banks = order, slots, banks
        self.filled = [ctx.enter_context(nc.semaphore(f"{name}_filled{n}")) for n in range(slots)]
        self.drained = [ctx.enter_context(nc.semaphore(f"{name}_drained{n}")) for n in range(slots)]

    def use(self, step, turn):
        names = [s for s, _ in self.order]
        if turn.j is None:
            n = sum(Turn(c).active(stage) for c in range(turn.c) for _, stage in self.order)
            n += sum(turn.active(stage) for _, stage in self.order[:names.index(step)])
            return n % self.slots, n // self.slots
        start = sum(Turn(c).active(stage) for c in range(STEADY) for _, stage in self.order)
        n = start + len(names) * (turn.c - STEADY) + names.index(step)
        return n % self.slots, turn.j * (2 * len(names) // self.slots) + n // self.slots


def hold(eng, sem, value):
    if not isinstance(value, int) or value > 0:
        eng.wait_ge(sem, value)


def hi_half(ap):
    return ap.bitcast(BF16).rearrange("p (n two) -> p n two", two=2)[:, :, 1]


def audio_tower(nc, io):
    ctx = ExitStack()
    with ctx:
        def sb(name, shape, dt=F32):
            return ctx.enter_context(nc.sbuf_tensor(name, shape, dt))

        def sem(name):
            return ctx.enter_context(nc.semaphore(name))

        const = sb("const", [128, CONST_KEPT])
        key_w = sb("key_w", [128, 128])
        qry_w = sb("qry_w", [128, 128])
        tok_v = sb("tok_v", [128, 1])
        tok_b = sb("tok_b", [128, 1])
        vplace = sb("vplace", [128, WIN, 32])
        a_hi = sb("a_hi", [128, HEADS, 2, C], F32R)
        a_lo = sb("a_lo", [128, HEADS, 2, C], F32R)
        o_w = sb("o_w", [128, HP, C])
        o_bias = sb("o_bias", [128, 1])
        g_whi = sb("g_whi", [128, 128], F32R)
        g_wlo = sb("g_wlo", [128, 128], F32R)
        g_b = sb("g_b", [128, 1])
        w1_hi = sb("w1_hi", [128, EXPERTS * HID], F32R)
        w1_lo = sb("w1_lo", [128, EXPERTS * HID], F32R)
        b1 = sb("b1", [128, 2 * EXPERTS])
        w2 = sb("w2", [128, 2 * EXPERTS, C])
        b2 = sb("b2", [128, EP])

        xin = sb("xin", [128, 2, 2, 2, C])
        xt = sb("xt", [128, 264])
        kq = sb("kq", [128, 2, 264])
        tanh = sb("tanh", [128, WIN, PADDED])
        sc = sb("sc", [128, 128])
        smax = sb("smax", [QUARTER, 8])
        sexp = sb("sexp", [QUARTER, 8, WIN])
        ssum = sb("ssum", [QUARTER, 8])
        srec = sb("srec", [QUARTER, 8])
        sn = sb("sn", [128, 4, 32])
        wt = sb("wt", [128, PADDED])
        band = sb("band", [128, 2, 2, 128])
        ht = sb("ht", [128, 2, TOKENS])
        stat = sb("stat", [HALF, 2, 8, 4])
        cen = sb("cen", [HALF, 4, C])
        sqr = sb("sqr", [HALF, 4, C])
        nn = sb("nn", [HALF, 2, 4, C])
        nhl = sb("nhl", [HALF, 4, 2 * C], F32R)
        nst = sb("nst", [128, 2, PAIR], F32R)
        g_hi = sb("g_hi", [128, 2, HEADS, PAIR], F32R)
        g_lo = sb("g_lo", [128, 2, HEADS, PAIR], F32R)
        mx = sb("mx", [128, 2, HEADS, 2])
        mneg = sb("mneg", [16, TOKENS], F32R)
        prob = sb("prob", [128, 4, 4 * TOKENS])
        ut = sb("ut", [128, 2, HP, TOKENS])
        den = sb("den", [16, TOKENS])
        rden = sb("rden", [128, TOKENS])
        pick = sb("pick", [128, 8, 128], BF16)
        room = sb("room", [128, 4, 8, C])
        room_flat = room[:, :, :, :].rearrange("p q e c -> p (q e c)")
        utn = room_flat[:, 0:2 * HP * TOKENS].rearrange("p (b h s) -> p b h s", b=2, h=HP)
        yw = room[0:HALF]
        h2t = sb("h2t", [128, TOKENS])
        h2 = sb("h2", [HALF, 2, 4, C])
        n2 = sqr
        n2hl = sb("n2hl", [HALF, 4, 2 * C], F32R)
        n2st = sb("n2st", [128, 2, PAIR], F32R)
        gt = sb("gt", [128, PAIR])
        lg = sb("lg", [HALF, 4, EXPERTS])
        gmax = sb("gmax", [HALF, 4])
        gexp = sb("gexp", [HALF, 4, EXPERTS])
        beats = sb("beats", [HALF, 4, EXPERTS, EXPERTS])
        duel = sb("duel", [HALF, 4, EXPERTS, EXPERTS])
        rank = sb("rank", [HALF, 4, EXPERTS])
        comb = sb("comb", [HALF, 2, 4, EXPERTS])
        hid = sb("hid", [128, 4, 2, PAIR])
        yt = sb("yt", [128, EP, PAIR])
        res = sb("res", [HALF, 2, 4, C])

        psum = ctx.enter_context(nc.psum_tensor("psum", [128, 8, 512], F32))
        big = Ring(nc, ctx, "big", BIG_ORDER, 2, 2)
        sums = Ring(nc, ctx, "sums", SUM_ORDER, 2, 1)
        tok = Ring(nc, ctx, "tok", TOK_ORDER, 1, 1)
        mid = Ring(nc, ctx, "mid", MID_ORDER, 1, 1)

        def big_ps(slot):
            return psum[:, 2 * slot:2 * slot + 2, :]

        def sum_ps(slot):
            return psum[:, 4 + slot, :]

        tok_ps, mid_ps = psum[:, 6, :], psum[:, 7, :]

        def cst(name, rows=128):
            a, b = CONSTS[name]
            return const[0:rows, a:b]

        ident = cst("ident")
        wq_in = prob[0:64, 0, 0:512]
        wk_in = prob[0:64, 1, 0:512]
        wv_in = prob[0:64, 2, 0:512]
        wo_in = prob[:, 3, 0:HP * C].rearrange("p (h c) -> p h c", h=HP)
        a_all = ut[:, 0, :, :].rearrange("p h s -> p (h s)")[:, 0:HEADS * C]
        wq_map = room_flat[:, 0:2 * HP * C].rearrange("p (h k c) -> p h k c", h=HP, k=2)
        wkv_map = room_flat[:, 2 * HP * C:4 * HP * C].rearrange("p (k h c) -> p k h c", k=2, h=HP)
        g_w = hid[:, 3, 0, 0:128]
        w1_in = hid[:, 0:3, :, :].rearrange("p a b n -> p (a b n)")[:, 0:EXPERTS * HID]

        zeroed = sem("zeroed")
        loaded = sem("loaded")
        w_mapped_pe = sem("w_mapped_pe")
        w_mapped = sem("w_mapped")
        x_loaded = [sem("x_loaded0"), sem("x_loaded1")]
        t_summed = sem("t_summed")
        tanh_done = sem("tanh_done")
        s_shifted = sem("s_shifted")
        s_exped = sem("s_exped")
        w_split = sem("w_split")
        s_normed = sem("s_normed")
        n_split = sem("n_split")
        den_loaded = [sem("den_loaded0"), sem("den_loaded1")]
        ut_done = sem("ut_done")
        den_inverted = sem("den_inverted")
        first_loaded = sem("first_loaded")
        g_hi_done = sem("g_hi_done")
        m_stored = [sem("m_stored0"), sem("m_stored1")]
        h2_ready = sem("h2_ready")
        n2_split = sem("n2_split")
        gate_shifted = sem("gate_shifted")
        gate_exped = sem("gate_exped")
        comb_ready = sem("comb_ready")
        y_summed = sem("y_summed")
        out_ready = sem("out_ready")
        out_stored = [sem("out_stored0"), sem("out_stored1")]
        dve_step = sem("dve_step")

        x_v = io["x"].rearrange("(j u b) (lt p) c -> j u p lt b c", u=2, b=2, p=128)
        out_v = io["out"].rearrange("(j u b) (half r) c -> j u r half b c", u=2, b=2, r=HALF)

        block = ctx.enter_context(nc.Block())
        N_LOADS, FIRST_LOADS = 19, 5

        def turns(eng, run, set_up=None):
            run(Turn(0))
            if set_up is not None:
                set_up()
            for c in range(1, LOOP_FROM):
                run(Turn(c))
            with eng.Fori(LOOP_FROM // 2, LOOP_TO // 2) as j:
                run(Turn(0, j))
                run(Turn(1, j))
            for c in range(LOOP_TO, TURNS):
                run(Turn(c))

        @block.sync
        def _(sp):
            sp.dma_start(const[:, :], io["const"][:, 0:CONST_KEPT]).then_inc(first_loaded, 16)
            sp.wait_ge(zeroed, 1)
            for w, name in ((key_w, "W_key"), (qry_w, "W_qry")):
                for b in range(2):
                    sp.dma_start(w[64 * b:64 * b + 64, 64 * b:64 * b + 64], io[name]).then_inc(first_loaded, 16)

            def set_up():
                loads = [(tok_b[0:64, :], io["b"]), (tok_b[64:128, :], io["b"]),
                         (wq_in, io["WQ"]), (wk_in, io["WK"]), (wv_in, io["WV"]),
                         (tok_v[0:64, :], io["v"]), (tok_v[64:128, :], io["v"]),
                         (vplace[:, :, :], io["const"][:, CONST_KEPT:].rearrange("p (r m) -> p r m", m=32)),
                         (wo_in, io["Wout"].rearrange("(h p) c -> p h c", p=128)),
                         (w1_in[0:64, :], io["W1T"]), (w1_in[64:128, :], io["W1T"]), (b1[:, :], io["b1T"]),
                         (o_bias[0:64, :], io["bout"]), (o_bias[64:128, :], io["bout"]),
                         (w2[:, :, :], io["W2T"]), (b2[:, :], io["b2T"]),
                         (g_w[0:64, 0:EXPERTS], io["WgT"]), (g_w[64:128, 0:EXPERTS], io["WgT"]),
                         (g_b[0:EXPERTS, :], io["bg"])]
                sp.wait_ge(zeroed, 2)
                for to, of in loads:
                    sp.dma_start(to, of).then_inc(loaded, 16)
                assert len(loads) == N_LOADS

            def dram(view, turn):
                if turn.j is None:
                    return view[turn.c // 2:turn.c // 2 + 1, turn.buf]
                return view[bass.ds(turn.j + turn.c // 2, 1), turn.buf]

            def run(turn):
                if turn.active(GLANCE):
                    p = turn.pair(GLANCE)
                    if turn.j is not None or p.c >= 2:
                        sp.wait_ge(tok.filled[0], tok.use("agg", turn.ago(1))[1] + 1)
                    for b in range(2):
                        sp.dma_start(xin[:, p.buf, :, b, :],
                                     dram(x_v, p)[:, :, :, b, :].rearrange("a p l c -> p (a l) c")
                                     ).then_inc(x_loaded[p.buf], 16)
                if turn.active(PEAK):
                    p = turn.pair(PEAK)
                    slot, n = tok.use("mt", turn)
                    sp.wait_ge(tok.drained[slot], n + 1)
                    sp.dma_start(g_hi[63:64, p.buf, :, :].bitcast(F32).rearrange("o h (b s) -> o (h b) s", b=2),
                                 mneg[:, :].bitcast(F32)).then_inc(m_stored[p.buf], 16)
                if turn.active(ATTEND):
                    p = turn.pair(ATTEND)
                    sp.wait_ge(ut_done, p.value(1, 1))
                    for par in range(2):
                        row = 64 * par + C - 1
                        sp.dma_start(den[8 * par:8 * par + 8, :],
                                     ut[row:row + 1, :, :, :].rearrange("o b h s -> o (b h) s")
                                     ).then_inc(den_loaded[p.buf], 16)
                if turn.active(MIX):
                    p = turn.pair(MIX)
                    sp.wait_ge(out_ready, p.value(1, 1))
                    for b in range(2):
                        sp.dma_start(dram(out_v, p)[:, :, :, b, :].rearrange("a r h c -> r (a h) c"),
                                     res[:, p.buf, :, :].rearrange("r (h b) c -> r h b c", b=2)[:, :, b, :]
                                     ).then_inc(out_stored[p.buf], 16)

            turns(sp, run, set_up)
            for n in range(2):
                sp.wait_ge(out_stored[n], 32 * (PAIRS // 2))

        @block.gpsimd
        def _(pool):
            def expert_sum(turn):
                p = turn.pair(MIX)
                for half in range(2):
                    slot, n = big.use(f"yn{half}", turn)
                    pool.wait_ge(big.drained[slot], n + 1)
                    q = yw[:, 2 * half:2 * half + 2]
                    step = p.value(8, 4 * half)
                    for i, width in enumerate((4, 2, 1)):
                        nc.gpsimd.tensor_tensor(q[:, :, 0:width, :], q[:, :, 0:width, :],
                                                q[:, :, width:2 * width, :], ALU.add).then_inc(y_summed, 1)
                        pool.wait_ge(y_summed, step + i + 1)
                    if half == 0:
                        hold(pool, out_stored[p.buf], p.rounds(32, 0))
                    last = nc.gpsimd.tensor_tensor(res[:, p.buf, 2 * half:2 * half + 2, :], q[:, :, 0, :],
                                                   h2[:, p.buf, 2 * half:2 * half + 2, :], ALU.add)
                    if half == 0:
                        last.then_inc(y_summed, 1)
                    else:
                        last.then_inc(out_ready, 1)
                        pool.wait_ge(out_ready, p.value(1, 1))
                        pool.sem_inc(y_summed, 1)

            def query_plus_key(turn):
                p = turn.pair(GLANCE)
                slot, n = tok.use("kq", turn)
                pool.wait_ge(tok.drained[slot], n + 1)
                if turn.active(WINDOW):
                    pool.wait_ge(tok.filled[0], tok.use("sc", turn)[1] + 1)
                rows = PADDED // WIN
                q = kq[:, 1, 0:PADDED].rearrange("p (a e) -> p a e", e=WIN)
                k = kq[:, 0, 0:PADDED + WIN].rearrange("p (a e) -> p a e", e=WIN)
                for r in range(WIN):
                    t = tanh[:, r, :].rearrange("p (a e) -> p a e", e=WIN)
                    last = nc.gpsimd.tensor_tensor(t[:, :, 0:r + 1], q[:, :, 0:r + 1],
                                                   k[:, 0:rows, r:r + 1].broadcast_to([128, rows, r + 1]),
                                                   ALU.add)
                    if r < WIN - 1:
                        nc.gpsimd.tensor_tensor(t[:, :, r + 1:WIN], q[:, :, r + 1:WIN],
                                                k[:, 1:rows + 1, r:r + 1].broadcast_to([128, rows, WIN - 1 - r]),
                                                ALU.add)
                last.then_inc(t_summed, 1)

            def run(turn):
                if turn.active(GLANCE):
                    query_plus_key(turn)
                if turn.active(MIX):
                    expert_sum(turn)

            turns(pool, run)

        @block.scalar
        def _(act):
            act.wait_ge(loaded, 16 * N_LOADS)

            def relu(turn, e):
                slot, n = big.use(f"l1_{e}", turn)
                if e >= 4:
                    if e % 2 == 0:
                        s, m = sums.use(f"l2_{(e - 4) // 2}", turn)
                        act.wait_ge(sums.filled[s], m + 1)
                elif e % 2 == 0 and turn.pair(MIX).active(GLANCE) and (turn.j is not None or turn.pair(MIX).c >= 1):
                    s, m = sums.use(f"l2_{2 + e // 2}", turn.ago(1))
                    act.wait_ge(sums.filled[s], m + 1)
                act.wait_ge(big.filled[slot], n + 1)
                for c in range(2):
                    last = nc.scalar.activation(hid[:, e % 4, c, :], big_ps(slot)[:, c, 0:PAIR], ACT.Relu,
                                                bias=b1[:, 2 * e + c:2 * e + c + 1])
                last.then_inc(big.drained[slot], 1)

            def expert_out(turn, ep):
                slot, n = sums.use(f"l2_{ep}", turn)
                if ep == 0 and (turn.j is not None or turn.pair(MIX).c >= 1):
                    s, m = big.use("yn1", turn.ago(1))
                    act.wait_ge(big.filled[s], m + 1)
                act.wait_ge(sums.filled[slot], n + 1)
                nc.scalar.activation(yt[:, ep, :], sum_ps(slot)[:, 0:PAIR], ACT.Identity,
                                     bias=b2[:, ep:ep + 1]).then_inc(sums.drained[slot], 1)

            def scores_exp(turn, i):
                p = turn.pair(ATTEND)
                slot, n = big.use(f"s{i}", turn)
                if i % 2 == 0 and (i >= 4 or turn.j is not None or p.c >= 1):
                    s, m = sums.use(f"av{(i // 2 + 2) % 4}", turn if i >= 4 else turn.ago(1))
                    act.wait_ge(sums.filled[s], m + 1)
                act.wait_ge(big.filled[slot], n + 1)
                nc.scalar.activation(prob[0:HALF, i % 4, :].rearrange("p (k n) -> p k n", k=2),
                                     big_ps(slot)[0:HALF, :, 0:PAIR], ACT.Exp).then_inc(big.drained[slot], 1)

            def attn_sums(turn, i):
                slot, n = sums.use(f"av{i}", turn)
                if i % 2 == 0 and turn.active(SETTLE):
                    s, m = big.use(f"rb{i // 2}", turn)
                    act.wait_ge(big.drained[s], m + 1)
                act.wait_ge(sums.filled[slot], n + 1)
                if i == HP - 1:
                    hold(act, den_inverted, turn.pair(ATTEND).value(1, 0))
                nc.scalar.activation(ut[:, i // 2, 2 * (i % 2):2 * (i % 2) + 2, :],
                                     sum_ps(slot)[:, 0:PAIR].rearrange("p (k n) -> p k n", k=2), ACT.Copy
                                     ).then_inc(sums.drained[slot], 1)
                if i == HP - 1:
                    s, m = sums.use("av2", turn)
                    act.wait_ge(sums.drained[s], m + 1)
                    act.wait_ge(sums.drained[slot], n + 1)
                    act.sem_inc(ut_done, 1)

            def window_exp(turn):
                act.wait_ge(s_shifted, turn.pair(WINDOW).value(1, 1))
                nc.scalar.activation(sexp[:, :, :], sexp[:, :, :], ACT.Exp).then_inc(s_exped, 1)

            def residual(turn):
                p = turn.pair(SETTLE)
                slot, n = mid.use("h2n", turn)
                hold(act, out_ready, p.value(1, -1))
                act.wait_ge(mid.filled[slot], n + 1)
                nc.scalar.activation(h2[:, p.buf, :, :].rearrange("p q c -> p (q c)"),
                                     mid_ps[0:HALF, 0:4 * C], ACT.Copy).then_inc(mid.drained[slot], 1)

            def norm1_cols(turn):
                p = turn.pair(WINDOW)
                if turn.j is not None or p.c >= 2:
                    s, m = big.use("s7", turn.ago(1))
                    act.wait_ge(big.filled[s], m + 1)
                slot, n = tok.use("nst", turn)
                act.wait_ge(tok.filled[slot], n + 1)
                nc.scalar.activation(nst[:, p.buf, :], tok_ps[:, 0:PAIR], ACT.Copy).then_inc(tok.drained[slot], 1)

            def norm2_cols(turn):
                p = turn.pair(SETTLE)
                slot, n = mid.use("n2st", turn)
                if turn.j is not None or p.c >= 2:
                    s, m = big.use("l1_7", turn.ago(1))
                    act.wait_ge(big.filled[s], m + 1)
                act.wait_ge(mid.filled[slot], n + 1)
                nc.scalar.activation(n2st[:, p.buf, :], mid_ps[:, 0:PAIR], ACT.Copy).then_inc(mid.drained[slot], 1)

            def gate_bias(turn):
                slot, n = mid.use("gate", turn)
                act.wait_ge(mid.filled[slot], n + 1)
                nc.scalar.activation(gt[:, :], mid_ps[:, 0:PAIR], ACT.Identity, bias=g_b[:, :]
                                     ).then_inc(mid.drained[slot], 1)

            def gate_exp(turn):
                act.wait_ge(gate_shifted, turn.pair(SETTLE).value(1, 1))
                nc.scalar.activation(gexp[:, :, :], gexp[:, :, :], ACT.Exp).then_inc(gate_exped, 1)

            def gram_hi(turn, g):
                p = turn.pair(GRAM)
                slot, n = big.use(f"g{g}", turn)
                if g == 0 and (turn.j is not None or p.c >= 2):
                    s, m = big.use("s7", turn.ago(1))
                    act.wait_ge(big.filled[s], m + 1)
                act.wait_ge(big.filled[slot], n + 1)
                nc.scalar.activation(g_hi[:, p.buf, 2 * g:2 * g + 2, :], big_ps(slot)[:, :, 0:PAIR], ACT.Copy
                                     ).then_inc(g_hi_done, 1)

            def window_tanh(turn):
                act.wait_ge(t_summed, turn.pair(GLANCE).value(1, 1))
                t = tanh[:, :, :].rearrange("p r w -> p (r w)")
                nc.scalar.activation(t, t, ACT.Tanh, bias=tok_b[:, :]).then_inc(tanh_done, 1)

            def maxima(turn):
                p = turn.pair(PEAK)
                slot, n = tok.use("mt", turn)
                if turn.j is not None or p.c >= 1:
                    act.wait_ge(m_stored[(p.c + 1) % 2], p.ago(1).rounds(16, 16))
                act.wait_ge(tok.filled[slot], n + 1)
                nc.scalar.activation(mneg[:, :], tok_ps[0:16, 0:TOKENS], ACT.Copy, scale=-1.0
                                     ).then_inc(tok.drained[slot], 1)

            def run(turn):
                win, glance, gram, peak = (turn.active(s) for s in (WINDOW, GLANCE, GRAM, PEAK))
                attend, settle, mix = turn.active(ATTEND), turn.active(SETTLE), turn.active(MIX)
                mix and relu(turn, 0)
                mix and relu(turn, 1)
                mix and relu(turn, 2)
                mix and relu(turn, 3)
                win and window_exp(turn)
                mix and expert_out(turn, 0)
                mix and relu(turn, 4)
                peak and maxima(turn)
                mix and relu(turn, 5)
                mix and expert_out(turn, 1)
                attend and scores_exp(turn, 0)
                attend and scores_exp(turn, 1)
                attend and scores_exp(turn, 2)
                settle and residual(turn)
                attend and scores_exp(turn, 3)
                mix and relu(turn, 6)
                attend and scores_exp(turn, 4)
                attend and scores_exp(turn, 5)
                attend and attn_sums(turn, 0)
                win and norm1_cols(turn)
                attend and attn_sums(turn, 1)
                mix and relu(turn, 7)
                gram and gram_hi(turn, 0)
                mix and expert_out(turn, 2)
                gram and gram_hi(turn, 1)
                mix and expert_out(turn, 3)
                settle and norm2_cols(turn)
                attend and scores_exp(turn, 6)
                settle and gate_bias(turn)
                attend and scores_exp(turn, 7)
                gram and gram_hi(turn, 2)
                gram and gram_hi(turn, 3)
                glance and window_tanh(turn)
                attend and attn_sums(turn, 2)
                settle and gate_exp(turn)
                attend and attn_sums(turn, 3)

            turns(act, run)

        @block.vector
        def _(dve):
            count = {"base": 0, "n": 0}

            def link(ins):
                count["n"] += 1
                ins.then_inc(dve_step, 1)
                dve.wait_ge(dve_step, count["base"] + count["n"])

            V = nc.vector
            V.memset(key_w[:, :], 0.0)
            V.memset(qry_w[:, :], 0.0).then_inc(zeroed, 1)
            for t in (wt[:, :], rden[:, :], xt[:, :], kq[:, :, :], sc[:, :], sn[:, :, :], g_w, g_b[:, :]):
                V.memset(t, 0.0)
            V.memset(nn[:, :, :, C - 1:C], 1.0).then_inc(zeroed, 1)
            dve.wait_ge(zeroed, 2)
            dve.wait_ge(first_loaded, 16 * FIRST_LOADS)
            def set_up():
                dve.wait_ge(loaded, 16 * N_LOADS)
                of = cst("pick").rearrange("p (k par o) -> p k par o", par=2, o=1)
                V.tensor_copy(pick[:, :, :].rearrange("p k (par c) -> p k par c", par=2),
                              of.broadcast_to([128, 8, 2, C]))
                V.tensor_scalar(vplace[:, :, :], vplace[:, :, :], tok_v[:, 0:1], None,
                                ALU.mult).then_inc(w_mapped, 1)
                for hi, lo, of in ((w1_hi, w1_lo, w1_in), (g_whi, g_wlo, g_w)):
                    link(V.tensor_copy(hi[:, :], of))
                    V.tensor_tensor(lo[:, :], of, hi[:, :], ALU.subtract).then_inc(w_mapped, 1)
                dve.wait_ge(w_mapped_pe, 1)
                V.tensor_copy(wq_map[:, :, :, :], psum[:, 0, 0:HP * C].rearrange("p (h o c) -> p h o c", h=HP, o=1)
                              .broadcast_to([128, HP, 2, C]))
                V.tensor_copy(wkv_map[:, :, :, :].rearrange("p k h c -> p (k h c)"), psum[:, 1, 0:2 * HP * C]
                              ).then_inc(w_mapped, 1)

            def set_up_products():
                dve.wait_ge(w_mapped_pe, 2)
                for par in range(2):
                    last = V.tensor_scalar(a_all.rearrange("p (h k c) -> p h k c", h=HP, k=2)[:, :, par, :],
                                           psum[:, 2 + par, 0:HP * C].rearrange("p (h c) -> p h c", h=HP),
                                           ATTN_SCALE, None, ALU.mult)
                link(last)
                a_twice = a_all.rearrange("p (h o c) -> p h o c", o=1, c=C).broadcast_to([128, HEADS, 2, C])
                link(V.tensor_copy(a_hi[:, :, :, :], a_twice))
                V.tensor_tensor(a_lo[:, :, :, :], a_twice, a_hi[:, :, :, :], ALU.subtract).then_inc(w_mapped, 1)
                for par in range(2):
                    last = V.tensor_copy(o_w[64 * par:64 * par + 64, :, :].rearrange("p h c -> p (h c)"),
                                         psum[64 * par:64 * par + 64, 4 + par, 0:HP * C])
                last.then_inc(w_mapped, 1)

            def layer_norm(which, src, to, width, freed=None):
                s = stat[:, which]
                c, q = cen[:, :, :], sqr[:, :, :]
                link(V.tensor_reduce(s[:, 0, :], src, AX.X, ALU.add))
                link(V.tensor_scalar(s[:, 1, :], s[:, 0, :], -1.0 / C, None, ALU.mult))
                ins = V.tensor_tensor(c, src, s[:, 1, :].rearrange("p (q o) -> p q o", o=1)
                                      .broadcast_to([HALF, 4, C]), ALU.add)
                if freed is None:
                    link(ins)
                else:
                    ins.then_inc(freed[0], 1)
                    dve.wait_ge(freed[0], freed[1])
                link(V.tensor_tensor(q, c, c, ALU.mult))
                link(V.tensor_reduce(s[:, 2, :], q, AX.X, ALU.add))
                link(V.tensor_scalar(s[:, 2, :], s[:, 2, :], 1.0 / C, EPS, ALU.mult, ALU.add))
                v, y, t = s[:, 2, :], s[:, 3, :], s[:, 4, :]
                link(V.tensor_single_scalar(y.bitcast(I32), v.bitcast(I32), 1, ALU.logical_shift_right))
                link(V.tensor_scalar(y.bitcast(I32), y.bitcast(I32), -1.0, float(RSQRT_GUESS), ALU.mult, ALU.add))
                for _ in range(3):
                    link(V.scalar_tensor_tensor(t, y, -0.5, y, ALU.mult, ALU.mult))
                    link(V.tensor_tensor(t, t, v, ALU.mult))
                    link(V.scalar_tensor_tensor(y, t, 1.5, y, ALU.add, ALU.mult))
                link(V.tensor_tensor(to[:, :, 0:width], c[:, :, 0:width],
                                     y.rearrange("p (q o) -> p q o", o=1).broadcast_to([HALF, 4, width]), ALU.mult))

            def pieces(t, rows):
                for n in range(2):
                    whole = t[32 * n:32 * n + rows, :]
                    ins = V.tensor_tensor(t[32 * n + 32:32 * n + 32 + rows, :], whole, hi_half(whole), ALU.subtract)
                    if n == 0:
                        link(ins)
                return ins

            def invert(turn):
                p = turn.pair(SETTLE)
                dve.wait_ge(den_loaded[p.buf], p.rounds(32, 32))
                if turn.j is not None or p.c >= 1:
                    s, m = big.use("rb1", turn.ago(1))
                    dve.wait_ge(big.filled[s], m + 1)
                link(V.reciprocal(rden[0:16, :], den[:, :]))
                pieces(rden, 16).then_inc(den_inverted, 1)

            def normalise(turn, b):
                if b == 0:
                    hold(dve, out_ready, turn.pair(MIX).value(1, 0))
                    if turn.j is not None or turn.pair(SETTLE).c >= 1:
                        dve.wait_ge(mid.filled[0], mid.use("op", turn.ago(1))[1] + 1)
                slot, n = big.use(f"rb{b}", turn)
                dve.wait_ge(big.filled[slot], n + 1)
                V.tensor_tensor(utn[:, b, :, :].rearrange("p (k r) s -> p k (r s)", k=2), big_ps(slot)[:, :, 0:PAIR],
                                ut[:, b, :, :].rearrange("p (k r) s -> p k (r s)", k=2), ALU.mult
                                ).then_inc(big.drained[slot], 1)

            def weigh(turn, half):
                p = turn.pair(MIX)
                slot, n = big.use(f"yn{half}", turn)
                if half == 0 and turn.active(SETTLE):
                    dve.wait_ge(mid.filled[0], mid.use("op", turn)[1] + 1)
                elif half == 0:
                    hold(dve, out_ready, p.value(1, 0))
                dve.wait_ge(comb_ready, p.value(1, 1))
                dve.wait_ge(big.filled[slot], n + 1)
                V.tensor_tensor(yw[:, 2 * half:2 * half + 2].rearrange("p q e c -> p (q e) c"),
                                big_ps(slot)[0:HALF].rearrange("p k (e c) -> p (k e) c", c=C),
                                comb[:, p.buf, 2 * half:2 * half + 2, :].rearrange("p q (e o) -> p (q e) o", o=1)
                                .broadcast_to([HALF, 16, C]), ALU.mult).then_inc(big.drained[slot], 1)

            def row_max(turn, i):
                four, b, st = i // 4, i // 2 % 2, i % 2
                slot, n = big.use(f"mx{i}", turn)
                if i == 0 and turn.active(PEAK):
                    dve.wait_ge(tok.filled[0], tok.use("mt", turn)[1] + 1)
                dve.wait_ge(big.filled[slot], n + 1)
                V.tensor_reduce(mx[:, st, 4 * four:4 * four + 4, b].rearrange("p (k h) -> p k h", k=2),
                                big_ps(slot)[:, :, 0:PAIR].rearrange("p k (h s) -> p k h s", h=2),
                                AX.X, ALU.max).then_inc(big.drained[slot], 1)

            def tok_copy(turn, step, to, of):
                slot, n = tok.use(step, turn)
                dve.wait_ge(tok.filled[slot], n + 1)
                V.tensor_copy(to, of).then_inc(tok.drained[slot], 1)

            def softmax_shift(turn):
                slot, n = tok.use("scn", turn)
                dve.wait_ge(tok.filled[slot], n + 1)
                s = (tok_ps[0:QUARTER, 0:128].rearrange("p (j m) -> p j m", m=32)[:, :, 0:2 * WIN]
                     .rearrange("p j (b r) -> p j b r", b=2))
                link(V.tensor_reduce(smax[:, :].rearrange("p (j b) -> p j b", b=2), s, AX.X, ALU.max))
                V.tensor_tensor(sexp[:, :, :].rearrange("p (j b) r -> p j b r", b=2), s,
                                smax[:, :].rearrange("p (j b o) -> p j b o", b=2, o=1)
                                .broadcast_to([QUARTER, 4, 2, WIN]), ALU.subtract).then_inc(tok.drained[slot], 1)
                dve.wait_ge(tok.drained[slot], n + 1)
                dve.sem_inc(s_shifted, 1)

            def softmax_norm(turn):
                dve.wait_ge(s_exped, turn.pair(WINDOW).value(1, 1))
                link(V.tensor_reduce(ssum[:, :], sexp[:, :, :], AX.X, ALU.add))
                link(V.reciprocal(srec[:, :], ssum[:, :]))
                V.tensor_tensor(sn[0:QUARTER, :, 0:2 * WIN].rearrange("p j (b r) -> p j b r", b=2),
                                sexp[:, :, :].rearrange("p (j b) r -> p j b r", b=2),
                                srec[:, :].rearrange("p (j b o) -> p j b o", b=2, o=1)
                                .broadcast_to([QUARTER, 4, 2, WIN]), ALU.mult).then_inc(s_normed, 1)

            def window_pieces(turn):
                if turn.j is not None or turn.pair(WINDOW).c >= 1:
                    dve.wait_ge(tok.filled[0], tok.use("rp", turn.ago(1))[1] + 1)
                slot, n = tok.use("et", turn)
                dve.wait_ge(tok.filled[slot], n + 1)
                V.tensor_copy(wt[0:32, :], tok_ps[0:32, 0:PADDED]).then_inc(tok.drained[slot], 1)
                dve.wait_ge(tok.drained[slot], n + 1)
                pieces(wt, 32).then_inc(w_split, 1)

            def band_weights(turn):
                slot, n = tok.use("rp", turn)
                dve.wait_ge(tok.filled[slot], n + 1)
                V.tensor_tensor(band[:, :, :, :].rearrange("p b t w -> p b (t w)"),
                                tok_ps[:, 0:512].rearrange("p (b w) -> p b w", b=2),
                                cst("band").rearrange("p (o w) -> p o w", o=1).broadcast_to([128, 2, 256]),
                                ALU.mult).then_inc(tok.drained[slot], 1)

            def residual(turn):
                slot, n = mid.use("op", turn)
                dve.wait_ge(mid.filled[slot], n + 1)
                V.scalar_tensor_tensor(h2t[:, :], mid_ps[:, 0:TOKENS], o_bias[:, 0:1],
                                       ht[:, turn.pair(SETTLE).buf, :], ALU.add, ALU.add
                                       ).then_inc(mid.drained[slot], 1)

            def window_out(turn):
                if turn.active(SETTLE):
                    slot, n = mid.use("op", turn)
                    dve.wait_ge(mid.drained[slot], n + 1)
                tok_copy(turn, "agg", ht[:, turn.pair(WINDOW).buf, :], tok_ps[:, 0:TOKENS])

            def norm1(turn):
                p = turn.pair(WINDOW)
                slot, n = tok.use("hn", turn)
                dve.wait_ge(tok.filled[slot], n + 1)
                if turn.j is not None or p.c >= 2:
                    s, m = sums.use("av3", turn.ago(1))
                    dve.wait_ge(sums.filled[s], m + 1)
                layer_norm(0, tok_ps[0:HALF, 0:4 * C].rearrange("p (q c) -> p q c", c=C), nn[:, p.buf], C - 1,
                           freed=(tok.drained[slot], n + 1))
                if turn.j is not None or p.c >= 1:
                    dve.wait_ge(tok.filled[0], tok.use("nst", turn.ago(1))[1] + 1)
                link(V.tensor_copy(nhl[:, :, 0:C], nn[:, p.buf]))
                V.tensor_tensor(nhl[:, :, C:2 * C], nn[:, p.buf], nhl[:, :, 0:C], ALU.subtract
                                ).then_inc(n_split, 1)

            def norm2(turn):
                p = turn.pair(SETTLE)
                slot, n = mid.use("h2n", turn)
                dve.wait_ge(mid.drained[slot], n + 1)
                layer_norm(1, h2[:, p.buf], n2, C)
                if turn.j is not None or p.c >= 1:
                    dve.wait_ge(mid.filled[0], mid.use("n2st", turn.ago(1))[1] + 1)
                link(V.tensor_copy(n2hl[:, :, 0:C], n2[:, :, :]))
                V.tensor_tensor(n2hl[:, :, C:2 * C], n2[:, :, :], n2hl[:, :, 0:C], ALU.subtract
                                ).then_inc(n2_split, 1)

            def gate_scores(turn):
                slot, n = mid.use("gaten", turn)
                dve.wait_ge(mid.filled[slot], n + 1)
                V.tensor_copy(lg[:, :, :], mid_ps[0:HALF, :].rearrange("p (q e) -> p q e", q=4)[:, :, 0:EXPERTS]
                              ).then_inc(mid.drained[slot], 1)
                dve.wait_ge(mid.drained[slot], n + 1)
                link(V.tensor_reduce(gmax[:, :], lg[:, :, :], AX.X, ALU.max))
                V.tensor_tensor(gexp[:, :, :], lg[:, :, :], gmax[:, :].rearrange("p (q o) -> p q o", o=1)
                                .broadcast_to([HALF, 4, EXPERTS]), ALU.subtract).then_inc(gate_shifted, 1)

            def gate_top2(turn):
                p = turn.pair(SETTLE)
                every = [HALF, 4, EXPERTS, EXPERTS]
                link(V.tensor_tensor(beats[:, :, :, :],
                                     lg[:, :, :].rearrange("p q (o e) -> p q o e", o=1).broadcast_to(every),
                                     lg[:, :, :].rearrange("p q (e o) -> p q e o", o=1).broadcast_to(every),
                                     ALU.is_ge))
                link(V.tensor_tensor(duel[:, :, :, :].rearrange("p q e f -> p q (e f)"),
                                     beats[:, :, :, :].rearrange("p q e f -> p q (e f)"),
                                     cst("lower", HALF).rearrange("p (o e) -> p o e", o=1)
                                     .broadcast_to([HALF, 4, EXPERTS * EXPERTS]), ALU.mult))
                link(V.tensor_tensor(beats[:, :, :, :], duel[:, :, :, :],
                                     duel[:, :, :, :].rearrange("p q e f -> p q f e"), ALU.subtract))
                link(V.tensor_reduce(rank[:, :, :], beats[:, :, :, :], AX.X, ALU.add))
                link(V.tensor_tensor(rank[:, :, :], rank[:, :, :],
                                     cst("rankmax", HALF).rearrange("p (o e) -> p o e", o=1)
                                     .broadcast_to([HALF, 4, EXPERTS]), ALU.is_lt))
                dve.wait_ge(gate_exped, p.value(1, 1))
                link(V.tensor_tensor(rank[:, :, :], rank[:, :, :], gexp[:, :, :], ALU.mult))
                link(V.tensor_reduce(gmax[:, :], rank[:, :, :], AX.X, ALU.add))
                link(V.reciprocal(gmax[:, :], gmax[:, :]))
                V.tensor_tensor(comb[:, p.buf], rank[:, :, :], gmax[:, :].rearrange("p (q o) -> p q o", o=1)
                                .broadcast_to([HALF, 4, EXPERTS]), ALU.mult).then_inc(comb_ready, 1)

            def gram_lo(turn, g):
                p = turn.pair(GRAM)
                slot, n = big.use(f"g{g}", turn)
                dve.wait_ge(g_hi_done, p.value(4, g + 1))
                V.tensor_tensor(g_lo[:, p.buf, 2 * g:2 * g + 2, :], big_ps(slot)[:, :, 0:PAIR],
                                g_hi[:, p.buf, 2 * g:2 * g + 2, :], ALU.subtract).then_inc(big.drained[slot], 1)

            def keys_queries(turn):
                hold(dve, t_summed, turn.pair(GLANCE).value(1, 0))
                tok_copy(turn, "kq", kq[:, :, 0:LENGTH], tok_ps[:, 0:512].rearrange("p (k n) -> p k n", k=2))

            def run(turn):
                win, glance, gram = turn.active(WINDOW), turn.active(GLANCE), turn.active(GRAM)
                settle, mix = turn.active(SETTLE), turn.active(MIX)
                win and tok_copy(turn, "sc", sc[:, 0:QUARTER], tok_ps[:, 0:QUARTER])
                settle and invert(turn)
                win and softmax_shift(turn)
                win and softmax_norm(turn)
                settle and normalise(turn, 0)
                settle and normalise(turn, 1)
                win and window_pieces(turn)
                win and band_weights(turn)
                settle and residual(turn)
                win and window_out(turn)
                win and norm1(turn)
                turn.c == 1 and turn.j is None and set_up_products()
                settle and norm2(turn)
                gram and gram_lo(turn, 0)
                gram and gram_lo(turn, 1)
                gram and row_max(turn, 0)
                glance and tok_copy(turn, "xt", xt[:, 0:LENGTH], tok_ps[:, 0:LENGTH])
                gram and row_max(turn, 1)
                mix and weigh(turn, 0)
                mix and weigh(turn, 1)
                glance and keys_queries(turn)
                gram and row_max(turn, 2)
                gram and row_max(turn, 3)
                gram and gram_lo(turn, 2)
                gram and gram_lo(turn, 3)
                gram and row_max(turn, 4)
                gram and row_max(turn, 5)
                settle and gate_scores(turn)
                gram and row_max(turn, 6)
                gram and row_max(turn, 7)
                settle and gate_top2(turn)

            def counted(turn):
                count["base"], count["n"] = count["base"] + count["n"], 0
                run(turn)

            counted(Turn(0))
            set_up()
            for c in range(1, LOOP_FROM):
                counted(Turn(c))
            start, per = count["base"] + count["n"], count["n"]
            with dve.Fori(LOOP_FROM // 2, LOOP_TO // 2) as j:
                for u in range(2):
                    count["base"], count["n"] = j * (2 * per) + (start - LOOP_FROM * per + u * per), 0
                    run(Turn(u, j))
                    assert count["n"] == per
            count["base"], count["n"] = start + (LOOP_TO - LOOP_FROM) * per, 0
            for c in range(LOOP_TO, TURNS):
                counted(Turn(c))

        @block.tensor
        def _(pe):
            mm = nc.tensor.matmul

            pe.wait_ge(zeroed, 2)
            pe.wait_ge(first_loaded, 16 * FIRST_LOADS)

            def set_up():
                pe.wait_ge(loaded, 16 * N_LOADS)
                for k, w in enumerate((wq_in, wk_in, wv_in)):
                    for hp in range(HP):
                        at = hp * C if k == 0 else ((k - 1) * HP + hp) * C
                        last = mm(psum[:, min(k, 1), at:at + C], w[:, 128 * hp:128 * hp + 128], cst("tmap", 64),
                                  start=True, stop=True)
                last.then_inc(w_mapped_pe, 1)

            def set_up_products():
                pe.wait_ge(w_mapped, 4)
                for par in range(2):
                    r = slice(64 * par, 64 * par + 64)
                    for hp in range(HP):
                        at = slice(hp * C, hp * C + C)
                        mm(psum[:, 2 + par, at], wq_map[r, hp].rearrange("p o c -> p (o c)"), wkv_map[r, 0, hp],
                           start=True, stop=True)
                        last = mm(psum[r, 4 + par, at], wkv_map[r, 1, hp], wo_in[r, hp, :], start=True, stop=True)
                last.then_inc(w_mapped_pe, 1)

            def flip(out, of):
                rows = of.shape[0]
                return nc.tensor.transpose(out, of, ident[0:rows, 0:rows])

            def free(ring, step, turn):
                slot, n = ring.use(step, turn)
                hold(pe, ring.drained[slot], n)
                return slot

            def ln_cols(q):
                at = (q % 2) * TOKENS + (q // 2) * HALF
                return slice(at, at + HALF)

            def inverses(turn, b):
                if b == 0:
                    pe.wait_ge(den_inverted, turn.pair(SETTLE).value(1, 1))
                slot = free(big, f"rb{b}", turn)
                for hp in range(HP):
                    last = mm(big_ps(slot)[:, hp // 2, TOKENS * (hp % 2):TOKENS * (hp % 2) + TOKENS],
                              pick[:, HP * b + hp, :], hi_half(rden[:, :]), start=True, stop=True)
                last.then_inc(big.filled[slot], 1)

            def layer1(turn, e):
                p = turn.pair(MIX)
                if e == 0:
                    pe.wait_ge(mid.drained[0], mid.use("n2st", turn.ago(1))[1] + 1)
                slot = free(big, f"l1_{e}", turn)
                for c in range(2):
                    at = slice((2 * e + c) * 128, (2 * e + c + 1) * 128)
                    for w in (w1_hi, w1_lo):
                        last = mm(big_ps(slot)[:, c, 0:PAIR], w[:, at], n2st[:, p.buf, :],
                                  start=(w is w1_hi), stop=(w is w1_lo))
                last.then_inc(big.filled[slot], 1)

            def layer2(turn, ep):
                for e in (2 * ep, 2 * ep + 1):
                    s, m = big.use(f"l1_{e}", turn)
                    pe.wait_ge(big.drained[s], m + 1)
                slot = free(sums, f"l2_{ep}", turn)
                for c in range(2):
                    for par in range(2):
                        e = 2 * ep + par
                        last = mm(sum_ps(slot)[64 * par:64 * par + 64, 0:PAIR], w2[:, 2 * e + c, :],
                                  hid[:, e % 4, c, :], start=(c == 0), stop=(c == 1))
                last.then_inc(sums.filled[slot], 1)

            def yn(turn, half):
                if half == 0:
                    for ep in (2, 3):
                        s, m = sums.use(f"l2_{ep}", turn)
                        pe.wait_ge(sums.drained[s], m + 1)
                slot = free(big, f"yn{half}", turn)
                for b in range(2):
                    for ep in range(EP):
                        last = flip(big_ps(slot)[0:HALF, b, 128 * ep:128 * ep + 128], yt[:, ep, ln_cols(2 * half + b)])
                last.then_inc(big.filled[slot], 1)

            def score(turn, i):
                p = turn.pair(ATTEND)
                b, four, tt = i // 4, i // 2 % 2, i % 2
                keys = slice(b * TOKENS + tt * HALF, b * TOKENS + (tt + 1) * HALF)
                if i == 0 and turn.pair(ATTEND).c == 0 and turn.j is None:
                    pe.wait_ge(w_mapped, 6)
                if i == 0:
                    pe.wait_ge(m_stored[p.buf], p.rounds(16, 16))
                slot = free(big, f"s{i}", turn)
                for k in range(2):
                    h = 4 * four + 2 * k
                    for g in (g_hi, g_lo):
                        last = mm(big_ps(slot)[0:HALF, k, 0:PAIR], nst[:, p.buf, keys],
                                  g[:, p.buf, h:h + 2, b * TOKENS:(b + 1) * TOKENS],
                                  start=(g is g_hi), stop=(g is g_lo))
                last.then_inc(big.filled[slot], 1)

            def attend_sum(turn, i):
                p = turn.pair(ATTEND)
                b = i // 2
                for tt in range(2):
                    s, m = big.use(f"s{2 * i + tt}", turn)
                    pe.wait_ge(big.drained[s], m + 1)
                slot = free(sums, f"av{i}", turn)
                for tt in range(2):
                    for par in range(2):
                        last = mm(sum_ps(slot)[64 * par:64 * par + 64, 0:PAIR], nn[:, p.buf, 2 * tt + b, :],
                                  prob[0:HALF, (2 * i + tt) % 4, :].rearrange("p (k r s) -> p k r s", k=2, r=2)[:, :, par, :],
                                  start=(tt == 0), stop=(tt == 1))
                last.then_inc(sums.filled[slot], 1)

            def row_max(turn, i):
                p = turn.pair(GRAM)
                four, b, st = i // 4, i // 2 % 2, i % 2
                if i % 4 == 0:
                    pe.wait_ge(g_hi_done, p.value(4, 2 * four + 2))
                slot = free(big, f"mx{i}", turn)
                for h in range(4):
                    at = b * TOKENS + st * (TOKENS - 128)
                    last = mm(big_ps(slot)[:, h // 2, TOKENS * (h % 2):TOKENS * (h % 2) + TOKENS],
                              hi_half(g_hi[:, p.buf, 4 * four + h, at:at + 128]),
                              hi_half(nst[:, p.buf, b * TOKENS:(b + 1) * TOKENS]), start=True, stop=True)
                last.then_inc(big.filled[slot], 1)

            def window_scores(turn):
                if turn.j is None and turn.c == 1:
                    pe.wait_ge(w_mapped, 1)
                pe.wait_ge(tanh_done, turn.pair(WINDOW).value(1, 1))
                free(tok, "sc", turn)
                for r in range(WIN):
                    for qt in range(4):
                        last = mm(tok_ps[32 * qt:32 * qt + 32, 0:QUARTER], vplace[:, r, :],
                                  tanh[:, r, QUARTER * qt:QUARTER * (qt + 1)], start=(r == 0), stop=(r == WIN - 1))
                last.then_inc(tok.filled[0], 1)

            def window_rows(turn):
                free(tok, "scn", turn)
                flip(tok_ps[:, 0:128], sc[:, :]).then_inc(tok.filled[0], 1)

            def window_weights(turn):
                pe.wait_ge(s_normed, turn.pair(WINDOW).value(1, 1))
                free(tok, "et", turn)
                for qt in range(4):
                    last = flip(tok_ps[0:32, QUARTER * qt:QUARTER * qt + 128], sn[:, qt, :])
                last.then_inc(tok.filled[0], 1)

            def window_spread(turn):
                free(tok, "rp", turn)
                pe.wait_ge(w_split, turn.pair(WINDOW).value(1, 1))
                spread = hi_half(cst("spread")).rearrange("p (b t l) -> p b t l", b=2, t=2)
                for b in range(2):
                    for lt in range(2):
                        w0 = lt * (TOKENS - 128)
                        last = mm(tok_ps[:, (2 * b + lt) * 128:(2 * b + lt + 1) * 128], spread[:, b, lt, :],
                                  hi_half(wt[:, w0:w0 + 128]), start=True, stop=True)
                last.then_inc(tok.filled[0], 1)

            def window_sum(turn):
                free(tok, "agg", turn)
                for lt in range(2):
                    w0 = lt * (TOKENS - 128)
                    for b in range(2):
                        last = mm(tok_ps[64 * b:64 * b + 64, w0:w0 + 128], xin[:, turn.pair(WINDOW).buf, lt, b, :],
                                  band[:, b, lt, :], start=(lt == 0), stop=(lt == 1), skip_group_check=True)
                last.then_inc(tok.filled[0], 1)

            def h_rows(turn):
                free(tok, "hn", turn)
                for half in range(2):
                    last = flip(tok_ps[0:HALF, 128 * half:128 * half + 128],
                                ht[:, turn.pair(WINDOW).buf, half * HALF:(half + 1) * HALF])
                last.then_inc(tok.filled[0], 1)

            def project(turn):
                for g in range(2):
                    s, m = big.use(f"rb{g}", turn)
                    pe.wait_ge(big.drained[s], m + 1)
                free(mid, "op", turn)
                for hp in range(HP):
                    for b in range(2):
                        last = mm(mid_ps[64 * b:64 * b + 64, 0:TOKENS], o_w[:, hp, :],
                                  utn[:, b, hp, :], start=(hp == 0), stop=(hp == HP - 1))
                last.then_inc(mid.filled[0], 1)

            def h2_rows(turn):
                free(mid, "h2n", turn)
                for half in range(2):
                    last = flip(mid_ps[0:HALF, 128 * half:128 * half + 128], h2t[:, half * HALF:(half + 1) * HALF])
                last.then_inc(mid.filled[0], 1)

            def norm1_cols(turn):
                pe.wait_ge(n_split, turn.pair(WINDOW).value(1, 1))
                free(tok, "nst", turn)
                for q in range(4):
                    last = flip(tok_ps[:, ln_cols(q)], nhl[:, q, :].bitcast(F32))
                last.then_inc(tok.filled[0], 1)

            def norm2_cols(turn):
                pe.wait_ge(n2_split, turn.pair(SETTLE).value(1, 1))
                free(mid, "n2st", turn)
                for q in range(4):
                    last = flip(mid_ps[:, ln_cols(q)], n2hl[:, q, :].bitcast(F32))
                last.then_inc(mid.filled[0], 1)

            def gate(turn):
                free(mid, "gate", turn)
                buf = turn.pair(SETTLE).buf
                mm(mid_ps[:, 0:PAIR], g_whi[:, :], n2st[:, buf, :], start=True, stop=False)
                mm(mid_ps[:, 0:PAIR], g_wlo[:, :], n2st[:, buf, :], start=False, stop=True
                   ).then_inc(mid.filled[0], 1)

            def gate_rows(turn):
                free(mid, "gaten", turn)
                for q in range(4):
                    last = flip(mid_ps[0:HALF, 128 * q:128 * (q + 1)], gt[:, ln_cols(q)])
                last.then_inc(mid.filled[0], 1)

            def gram(turn, g):
                if g == 0 and turn.j is None and turn.c == 1:
                    pe.wait_ge(w_mapped, 5)
                if g == 0:
                    pe.wait_ge(tok.drained[0], tok.use("nst", turn)[1] + 1)
                slot = free(big, f"g{g}", turn)
                for k in range(2):
                    for w in (a_hi, a_lo):
                        last = mm(big_ps(slot)[:, k, 0:PAIR], w[:, 2 * g + k, :, :].rearrange("p o c -> p (o c)"),
                                  nst[:, turn.pair(GRAM).buf, :], start=(w is a_hi), stop=(w is a_lo))
                last.then_inc(big.filled[slot], 1)

            def x_cols(turn):
                p = turn.pair(GLANCE)
                pe.wait_ge(x_loaded[p.buf], p.rounds(32, 32))
                free(tok, "xt", turn)
                for lt in range(2):
                    last = flip(tok_ps[:, 128 * lt:128 * lt + 128],
                                xin[:, p.buf, lt, :, :].rearrange("p b c -> p (b c)"))
                last.then_inc(tok.filled[0], 1)

            def keys_queries(turn):
                free(tok, "kq", turn)
                mm(tok_ps[:, 0:LENGTH], key_w[:, :], xt[:, 0:LENGTH], start=True, stop=True)
                mm(tok_ps[:, LENGTH:2 * LENGTH], qry_w[:, :], xt[:, WIN // 2:WIN // 2 + LENGTH],
                   start=True, stop=True).then_inc(tok.filled[0], 1)

            def maxima(turn):
                for i in (6, 7):
                    s, m = big.use(f"mx{i}", turn.ago(1))
                    pe.wait_ge(big.drained[s], m + 1)
                free(tok, "mt", turn)
                for st in range(2):
                    at = st * (TOKENS - 128)
                    last = flip(tok_ps[0:16, at:at + 128], mx[:, st].rearrange("p h b -> p (h b)"))
                last.then_inc(tok.filled[0], 1)

            def run(turn):
                win, glance, gram_on, peak = (turn.active(s) for s in (WINDOW, GLANCE, GRAM, PEAK))
                attend, settle, mix = turn.active(ATTEND), turn.active(SETTLE), turn.active(MIX)
                win and window_scores(turn)
                mix and layer1(turn, 0)
                mix and layer1(turn, 1)
                mix and layer1(turn, 2)
                mix and layer1(turn, 3)
                win and window_rows(turn)
                mix and layer2(turn, 0)
                mix and layer1(turn, 4)
                settle and inverses(turn, 0)
                mix and layer2(turn, 1)
                settle and inverses(turn, 1)
                peak and maxima(turn)
                mix and layer1(turn, 5)
                win and window_weights(turn)
                settle and project(turn)
                win and window_spread(turn)
                attend and score(turn, 0)
                attend and score(turn, 1)
                win and window_sum(turn)
                attend and score(turn, 2)
                win and h_rows(turn)
                turn.c == 1 and turn.j is None and set_up_products()
                settle and h2_rows(turn)
                attend and score(turn, 3)
                mix and layer1(turn, 6)
                attend and attend_sum(turn, 0)
                attend and score(turn, 4)
                attend and score(turn, 5)
                attend and attend_sum(turn, 1)
                win and norm1_cols(turn)
                mix and layer1(turn, 7)
                gram_on and gram(turn, 0)
                mix and layer2(turn, 2)
                gram_on and gram(turn, 1)
                mix and layer2(turn, 3)
                gram_on and row_max(turn, 0)
                settle and norm2_cols(turn)
                attend and score(turn, 6)
                glance and x_cols(turn)
                gram_on and row_max(turn, 1)
                settle and gate(turn)
                mix and yn(turn, 0)
                mix and yn(turn, 1)
                glance and keys_queries(turn)
                attend and score(turn, 7)
                gram_on and row_max(turn, 2)
                settle and gate_rows(turn)
                gram_on and row_max(turn, 3)
                gram_on and gram(turn, 2)
                gram_on and gram(turn, 3)
                attend and attend_sum(turn, 2)
                gram_on and row_max(turn, 4)
                gram_on and row_max(turn, 5)
                attend and attend_sum(turn, 3)
                gram_on and row_max(turn, 6)
                gram_on and row_max(turn, 7)

            turns(pe, run, set_up)


def constants():
    out = np.zeros((128, CONST_COLS), np.float32)

    def put(name, a):
        lo, hi = CONSTS[name]
        out[:a.shape[0], lo:hi] = a.reshape(a.shape[0], -1)

    put("ident", np.eye(128, dtype=np.float32))
    p, lt, w = np.ogrid[0:128, 0:2, 0:128]
    reach = (128 * lt + p) - ((TOKENS - 128) * lt + w)
    put("band", ((reach >= 0) & (reach < WIN)).astype(np.float32))
    row, b, lt, p = np.ogrid[0:128, 0:2, 0:2, 0:128]
    put("spread", ((row % 32 == b * WIN + (128 * lt + p) % WIN) & (row < 96)).astype(np.float32))
    row, k, par = np.ogrid[0:128, 0:8, 0:2]
    put("pick", ((row % 32 == 8 * par + k) & (row < 96)).astype(np.float32))
    tmap = np.eye(C, dtype=np.float32)
    tmap[C - 1, :] = -1.0
    tmap[:, C - 1] = 0.0
    put("tmap", tmap)
    e, f = np.ogrid[0:EXPERTS, 0:EXPERTS]
    put("lower", np.broadcast_to((f < e).astype(np.float32), (128, EXPERTS, EXPERTS)))
    put("rankmax", np.broadcast_to(np.arange(EXPERTS, dtype=np.float32) - (EXPERTS - 1 - 2), (128, EXPERTS)))
    row, r, m = np.ogrid[0:128, 0:WIN, 0:32]
    put("vplace", (m == (row // 64) * WIN + r).astype(np.float32))
    return out


def kernel(x, L0_tok_W_qry, L0_tok_W_key, L0_tok_v, L0_tok_b, L0_attn_WQ, L0_attn_WK, L0_attn_WV, L0_attn_Wout,
           L0_attn_bout, L0_ffn_Wg, L0_ffn_bg, L0_ffn_W1, L0_ffn_b1, L0_ffn_W2, L0_ffn_b2):
    import concourse.bacc as bacc
    from concourse.bass_utils import run_bass_kernel_spmd

    def lay(a, axes=None, shape=None):
        a = np.asarray(a)
        a = a if axes is None else a.transpose(axes)
        return np.ascontiguousarray(a if shape is None else a.reshape(shape))

    col = (-1, 1)
    arrays = {
        "x": lay(x), "W_qry": lay(L0_tok_W_qry), "W_key": lay(L0_tok_W_key), "v": lay(L0_tok_v, None, col),
        "b": lay(L0_tok_b, None, col), "WQ": lay(L0_attn_WQ), "WK": lay(L0_attn_WK), "WV": lay(L0_attn_WV),
        "Wout": lay(L0_attn_Wout), "bout": lay(L0_attn_bout, None, col),
        "WgT": lay(L0_ffn_Wg, (1, 0)), "bg": lay(L0_ffn_bg, None, col),
        "W1T": lay(L0_ffn_W1, (2, 0, 1), (C, EXPERTS * HID)),
        "b1T": lay(np.asarray(L0_ffn_b1).reshape(2 * EXPERTS, 128), (1, 0)),
        "W2T": lay(np.asarray(L0_ffn_W2).reshape(EXPERTS, C, 2, 128), (3, 0, 2, 1), (128, 2 * EXPERTS, C)),
        "b2T": lay(np.asarray(L0_ffn_b2).reshape(EP, 128), (1, 0)),
        "const": constants(),
    }
    nc = bacc.Bacc("TRN2", target_bir_lowering=False, num_devices=1)
    io = {name: nc.dram_tensor(f"in_{name}", a.shape, F32, kind="ExternalInput").ap() for name, a in arrays.items()}
    io["out"] = nc.dram_tensor("out", (BATCH, TOKENS, C), F32, kind="ExternalOutput").ap()
    audio_tower(nc, io)
    r = run_bass_kernel_spmd(nc, [{f"in_{name}": a for name, a in arrays.items()}], core_ids=[0])
    return r.results[0]["out"]
```
